# Optimizing a Trainium2 kernel written in Bass

```python
import numpy as np
import jax
import jax.numpy as jnp

def _softmax(x, axis=-1):
    return jax.nn.softmax(x, axis=axis)
def _gelu(x):
    return jax.nn.gelu(x, approximate=True)
def _silu(x):
    return jax.nn.silu(x)
def _sigmoid(x):
    return jax.nn.sigmoid(x)
def _layernorm(x, axis=-1, eps=1e-5):
    m = jnp.mean(x, axis=axis, keepdims=True)
    v = jnp.var(x, axis=axis, keepdims=True)
    return (x - m) / jnp.sqrt(v + eps)
def _scatter_add(tgt, idx, src, axis=0):
    return tgt.at[idx].add(src)
def _segment_sum(src, seg, n):
    return jax.ops.segment_sum(src, seg, n)

kernel_name = 'mk_metaformer_d1_conv_nhwc128_2e5e94'

def setup_inputs(seed: int = 0):
    np.random.seed(seed)
    _w = jnp.asarray
    def _rec_inputs():
        import jax
        import jax.numpy as jnp
        _gk = jax.random.key(seed)
        x = -0.000125 + 0.9999 * jax.random.normal(jax.random.fold_in(_gk, 1), (16, 128, 128, 128), jnp.float32)
        return x
    x = _rec_inputs()
    def _L0_conv_setup():
        import jax, jax.numpy as jnp
        import numpy as np
        DIM = 128
        WS = 4
        NUM_HEADS = 4
        key = jax.random.key(seed)
        k1, k2, k3, k4 = jax.random.split(key, 4)
        x = jax.random.normal(k1, (16, 128, 128, DIM), dtype=jnp.float32)
        w_qkv = jax.random.normal(k2, (DIM, 3 * DIM), dtype=jnp.float32) * (1.0 / np.sqrt(DIM))
        w_proj = jax.random.normal(k3, (DIM, DIM), dtype=jnp.float32) * (1.0 / np.sqrt(DIM))
        b_proj = jax.random.normal(k4, (DIM,), dtype=jnp.float32) * 0.01
        return {'x': x, 'w_qkv': w_qkv, 'w_proj': w_proj, 'b_proj': b_proj}
    _L0_conv_all = _L0_conv_setup()
    _L0_conv_in = {k: v for k, v in _L0_conv_all.items() if k in ('w_qkv', 'w_proj', 'b_proj', )}
    del _L0_conv_all

    def _L0_ffn_setup():
        import jax, jax.numpy as jnp
        import numpy as np
        B, S, D, E, H, O, K = (512, 2048, 128, 64, 512, 128, 8)
        key = jax.random.key(seed)
        k0, k1, k2, k3 = jax.random.split(key, 4)
        x = jax.random.normal(k0, (B, S, D), dtype=jnp.float32)
        gate_w = jax.random.normal(k1, (E, D), dtype=jnp.float32) * (1.0 / np.sqrt(D))
        gate_b = jnp.zeros((E,), dtype=jnp.float32)
        weight1 = jax.random.uniform(k2, (E, D + 1, H), dtype=jnp.float32, minval=-1.0, maxval=1.0) * (1.0 / np.sqrt(D + 1))
        weight2 = jax.random.uniform(k3, (E, H + 1, O), dtype=jnp.float32, minval=-1.0, maxval=1.0) * (1.0 / np.sqrt(H + 1))
        return {'x': x, 'gate_w': gate_w, 'gate_b': gate_b, 'weight1': weight1, 'weight2': weight2}
    _L0_ffn_all = _L0_ffn_setup()
    _L0_ffn_in = {k: v for k, v in _L0_ffn_all.items() if k in ('gate_w', 'gate_b', 'weight1', 'weight2', )}
    del _L0_ffn_all

    return {
        "x": x,
        "L0_conv_w_qkv": _L0_conv_in["w_qkv"],
        "L0_conv_w_proj": _L0_conv_in["w_proj"],
        "L0_conv_b_proj": _L0_conv_in["b_proj"],
        "L0_ffn_gate_w": _L0_ffn_in["gate_w"],
        "L0_ffn_gate_b": _L0_ffn_in["gate_b"],
        "L0_ffn_weight1": _L0_ffn_in["weight1"],
        "L0_ffn_weight2": _L0_ffn_in["weight2"],
    }

def reference(x, L0_conv_w_qkv, L0_conv_w_proj, L0_conv_b_proj, L0_ffn_gate_w, L0_ffn_gate_b, L0_ffn_weight1, L0_ffn_weight2):
    import jax
    import jax.numpy as jnp
    def _L0_conv_ref(x, w_qkv, w_proj, b_proj):
        import jax, jax.numpy as jnp
        import numpy as np
        DIM = 128
        WS = 4
        NUM_HEADS = 4
        B, H, W, C = x.shape
        ws, nheads = (WS, NUM_HEADS)
        hd = C // nheads
        nh, nw = (H // ws, W // ws)
        T = ws * ws
        xw = x.reshape(B, nh, ws, nw, ws, C).transpose(0, 1, 3, 2, 4, 5)
        xw = xw.reshape(B * nh * nw, T, C)
        qkv = xw @ w_qkv
        q, k, v = jnp.split(qkv, 3, axis=-1)
        q = q.reshape(-1, T, nheads, hd)
        k = k.reshape(-1, T, nheads, hd)
        v = v.reshape(-1, T, nheads, hd)
        scale = 1.0 / np.sqrt(hd)
        attn = jnp.einsum('nqhd,nkhd->nhqk', q, k) * scale
        attn = jax.nn.softmax(attn, axis=-1)
        out = jnp.einsum('nhqk,nkhd->nqhd', attn, v).reshape(-1, T, C)
        out = out @ w_proj + b_proj
        out = out.reshape(B, nh, nw, ws, ws, C).transpose(0, 1, 3, 2, 4, 5)
        return out.reshape(B, H, W, C)

    def _L0_ffn_ref(x, gate_w, gate_b, weight1, weight2):
        import jax, jax.numpy as jnp
        import numpy as np
        B, S, D, E, H, O, K = (512, 2048, 128, 64, 512, 128, 8)
        Bn, Sn, Dn = x.shape
        logits = jnp.einsum('bsd,ed->bse', x, gate_w) + gate_b
        probs = jax.nn.softmax(logits, axis=1)
        vals, idx = jax.lax.top_k(probs.transpose(0, 2, 1), K)
        topv = vals.transpose(0, 2, 1)
        topi = idx.transpose(0, 2, 1)
        flat_idx = topi.reshape(Bn, K * E)
        gathered = jnp.take_along_axis(x, flat_idx[:, :, None], axis=1)
        gathered = gathered.reshape(Bn, K, E, Dn)
        pooled = jnp.einsum('bked,bke->bed', gathered, topv)
        ones = jnp.ones((E, Bn, 1), dtype=x.dtype)
        h = jnp.concatenate([pooled.transpose(1, 0, 2), ones], axis=-1)
        h = jax.nn.gelu(jnp.einsum('ebd,edh->ebh', h, weight1), approximate=False)
        h = jnp.concatenate([h, ones], axis=-1)
        out = jnp.einsum('ebh,eho->ebo', h, weight2)
        out = out.transpose(1, 0, 2)
        weighted = jnp.einsum('beo,bke->bkeo', out, topv).reshape(Bn, K * E, O)
        outputs = jnp.zeros((Bn, Sn, O), dtype=x.dtype)
        outputs = outputs.at[jnp.arange(Bn)[:, None], flat_idx].add(weighted)
        return outputs

    def _gn(v, G=32, eps=1e-5):
        B_, H_, W_, C_ = v.shape
        g = v.reshape(B_, H_, W_, G, C_ // G)
        m = jnp.mean(g, axis=(1, 2, 4), keepdims=True)
        s = jnp.var(g, axis=(1, 2, 4), keepdims=True)
        return ((g - m) / jnp.sqrt(s + eps)).reshape(v.shape)

    def _ln_c(v, eps=1e-6):
        m = jnp.mean(v, axis=-1, keepdims=True)
        s = jnp.var(v, axis=-1, keepdims=True)
        return (v - m) / jnp.sqrt(s + eps)

    def _ln_t(v, eps=1e-5):
        m = jnp.mean(v, axis=-1, keepdims=True)
        s = jnp.var(v, axis=-1, keepdims=True)
        return (v - m) / jnp.sqrt(s + eps)

    def _to_tokens(v):
        B_, H_, W_, C_ = v.shape
        return v.reshape(B_, H_ * W_, C_)
    def _from_tokens(t, like):
        return t.reshape(like.shape)

    x = x + _L0_conv_ref(_ln_c(x), L0_conv_w_qkv, L0_conv_w_proj, L0_conv_b_proj)
    t = _to_tokens(x)
    t = t + _L0_ffn_ref(_ln_t(t), L0_ffn_gate_w, L0_ffn_gate_b, L0_ffn_weight1, L0_ffn_weight2)
    x = _from_tokens(t, x)
    return x


_drawn_inputs = setup_inputs


def setup_inputs(seed=0):
    import zlib

    import numpy as np

    out = dict(_drawn_inputs(seed))
    spreads = {'L0_ffn_gate_b': (0.0, 0.1)}
    factors = {'L0_conv_b_proj': 5.889,
     'L0_ffn_gate_w': 8.0,
     'L0_ffn_weight1': 8.0,
     'L0_ffn_weight2': 8.0}
    for name, (base, spread) in spreads.items():
        noise = np.random.default_rng([zlib.crc32(name.encode()), seed]).standard_normal(out[name].shape)
        drawn = base * np.exp(spread * noise) if base else spread * noise
        out[name] = jnp.asarray(drawn.astype(out[name].dtype))
    for name, factor in factors.items():
        out[name] = (out[name] * factor).astype(out[name].dtype)
    return out
```

```python
from contextlib import ExitStack

import concourse.bass as bass
from concourse import mybir

F32 = mybir.dt.float32
BF16 = mybir.dt.bfloat16
U32 = mybir.dt.uint32
ALU = mybir.AluOpType
ACT = mybir.ActivationFunctionType
X = mybir.AxisListType.X

P = 128
MASKED = -1e30
XT, QKV, SC, SM, PT, PV, ADD, LN2, GATE = 1, 2, 3, 4, 5, 6, 7, 8, 9


def metaformer_layer(nc, x, w_qkv, w_proj, b_proj, gate_w, gate_b, weight1, weight2, out):
    B, HH, WW, C = x.shape
    E, _, HID = weight1.shape
    HEADS = 4
    HD = C // HEADS
    J = 4
    BT = P * J
    S = HH * WW
    NBLK = B * S // BT
    CH = 8
    NCH = NBLK // CH
    QCH = NCH // B
    G = BT // 32
    K8 = 8
    PAIRS = B // 2
    NE = E // 8
    RING = 16
    SCALE = float(HD) ** -0.5
    assert C == P and E == 64 and HID == 4 * P and BT == 4 * WW and NBLK == CH * NCH

    x_blk = x.rearrange("b h w c -> (b h w) c").rearrange("(n p j) c -> n p (j c)", p=P, j=J)
    out_rows = out.rearrange("b h w c -> (b h w) c")
    out_blk = out_rows.rearrange("(n p j) c -> n p (j c)", p=P, j=J)
    expert_dram = nc.dram_tensor("expert_rows", (B, E, C), F32, kind="Internal").ap()

    ctx = ExitStack()
    with ctx:
        def sb(name, shape, dt=F32):
            return ctx.enter_context(nc.sbuf_tensor(name, shape, dt))

        def sem(name):
            return ctx.enter_context(nc.semaphore(name))

        arena_a = sb("arena_a", [P, 8192])
        arena_b = sb("arena_b", [P, 8192])
        arena_c = sb("arena_c", [P, 4096])
        arena_d = sb("arena_d", [P, 2048])
        xin = [arena_d[:, 512 * i:512 * i + 512] for i in range(4)]
        xt = [arena_a[:, 512 * i:512 * i + 512] for i in range(8)]
        kbd = [arena_a[:, 4096 + 2048 * i:6144 + 2048 * i] for i in range(2)]
        pbd = [arena_b[:, 2048 * i:2048 * i + 2048] for i in range(2)]
        xn = [arena_b[:, 4096 + 512 * i:4608 + 512 * i] for i in range(2)]
        xnT = [arena_b[:, 5120 + 512 * i:5632 + 512 * i] for i in range(2)]
        qT = [arena_b[:, 6144 + 512 * i:6656 + 512 * i] for i in range(2)]
        kT = [arena_b[:, 7168 + 512 * i:7680 + 512 * i] for i in range(2)]
        v = [arena_c[:, 512 * i:512 * i + 512] for i in range(4)]
        pr = [arena_c[:, 2048 + 512 * i:2560 + 512 * i] for i in range(2)]
        pT = [arena_c[:, 3072 + 512 * i:3584 + 512 * i] for i in range(2)]
        gathered = arena_a[:, :].rearrange("p (n c) -> p n c", c=C)
        wsel = arena_b[:, :].rearrange("p (b n) -> p b n", b=PAIRS)
        onehot = arena_c[:, :].rearrange("p (n m) -> p n m", m=64)

        oT = [sb(f"oT{i}", [P, 512]) for i in range(2)]
        tn = [sb(f"tn{i}", [P, 512]) for i in range(2)]
        tnT = [sb(f"tnT{i}", [P, 512]) for i in range(2)]
        logits = sb("logits", [P, CH * 256])
        early = sb("early", [P, 1024])
        w_sb = sb("w_sb", [P, 3 * C])
        wp_sb = sb("wp_sb", [P, C])
        bp_sb = sb("bp_sb", [P, C])
        gw_in = sb("gw_in", [E, C])
        gwT = sb("gwT", [P, E])
        gb2 = sb("gb2", [P, 1])
        ident = sb("ident", [P, P])
        mask_q = sb("mask_q", [P, P], BF16)
        mask_k = sb("mask_k", [P, 512], BF16)
        eps8 = sb("eps8", [P, 8])
        minus_half = sb("minus_half", [P, 64])
        half = sb("half", [P, 1])
        raw = [sb(f"raw{i}", [P, 8, 6]) for i in range(2)]
        mean2 = [sb(f"mean2{i}", [P, 8]) for i in range(2)]
        mdiff = sb("mdiff", [P, 8])
        mdiff2 = sb("mdiff2", [P, 8])
        csum = sb("csum", [P, 8])
        cvar = sb("cvar", [P, 8])
        vareps = [sb(f"vareps{i}", [P, 8]) for i in range(2)]
        rstd = [sb(f"rstd{i}", [P, 8]) for i in range(2)]
        nmr = [sb(f"nmr{i}", [P, 8]) for i in range(2)]
        mx = [sb(f"mx{i}", [P, G]) for i in range(2)]
        sm = [sb(f"sm{i}", [P, G]) for i in range(2)]
        rc = [sb(f"rc{i}", [P, G]) for i in range(2)]
        v8 = sb("v8", [P, 8])
        i8 = sb("i8", [P, 8], U32)
        negm = sb("negm", [P, 1])
        vals = sb("vals", [P, NCH * 8])
        toks = sb("toks", [P, NCH * 8])
        sums = sb("sums", [P, NCH])
        b1_in = sb("b1_in", [E, HID])
        b1T = sb("b1T", [P, J, E])
        b2_sb = sb("b2_sb", [P, C])
        w1r = sb("w1r", [P, RING, HID])
        w2r = sb("w2r", [P, RING, HID])

        bank = [ctx.enter_context(nc.psum_tensor(f"bank{i}", [P, 512], F32)) for i in range(8)]
        ps_x, ps_q, ps_k, ps_v, ps_s, ps_o, ps_y, ps_t = bank

        x_loaded = [sem(f"x_loaded{i}") for i in range(4)]
        stored = [sem(f"stored{i}") for i in range(8)]
        kbd_moved = [sem(f"kbd_moved{i}") for i in range(2)]
        pbd_moved = [sem(f"pbd_moved{i}") for i in range(2)]
        consts_loaded = sem("consts_loaded")
        consts_set = sem("consts_set")
        ident_zero = sem("ident_zero")
        mask_zero = sem("mask_zero")
        half_set = sem("half_set")
        exp_primed = sem("exp_primed")
        zeroed = sem("zeroed")
        gw_turned = sem("gw_turned")
        gwT_ready = sem("gwT_ready")
        raw_ready = sem("raw_ready")
        mdiff_ready = sem("mdiff_ready")
        mdiff2_ready = sem("mdiff2_ready")
        csum_ready = sem("csum_ready")
        cvar_ready = sem("cvar_ready")
        var_ready = sem("var_ready")
        rstd_ready = sem("rstd_ready")
        nmr_ready = sem("nmr_ready")
        xn_ready = sem("xn_ready")
        xb_ready = sem("xb_ready")
        x_turned = sem("x_turned")
        xnT_ready = sem("xnT_ready")
        k_done = sem("k_done")
        q_done = sem("q_done")
        v_done = sem("v_done")
        kT_ready = sem("kT_ready")
        qT_ready = sem("qT_ready")
        v_ready = sem("v_ready")
        scored = sem("scored")
        mx_ready = sem("mx_ready")
        shifted = sem("shifted")
        exp_done = sem("exp_done")
        sm_ready = sem("sm_ready")
        rc_ready = sem("rc_ready")
        p_normed = sem("p_normed")
        pT_ready = sem("pT_ready")
        pv_done = sem("pv_done")
        oT_ready = sem("oT_ready")
        y_done = sem("y_done")
        t_ready = sem("t_ready")
        tn_ready = sem("tn_ready")
        t_turned = sem("t_turned")
        tnT_ready = sem("tnT_ready")
        gate_done = sem("gate_done")
        l_ready = sem("l_ready")
        v8_ready = sem("v8_ready")
        i8_ready = sem("i8_ready")
        negm_ready = sem("negm_ready")
        early_copied = sem("early_copied")
        chunk_kept = sem("chunk_kept")
        chunk_summed = sem("chunk_summed")
        w1_loaded = [sem(f"w1_loaded{i}") for i in range(RING)]
        w2_loaded = [sem(f"w2_loaded{i}") for i in range(RING)]
        biases_loaded = sem("biases_loaded")

        def slots(eng, step):
            for n in range(2 * CH):
                step(n, n % CH, lambda k, n=n: 0 <= n - k < NBLK, None)
            with eng.Fori(0, NCH - 2) as c:
                for u in range(CH):
                    step(CH * c + (2 * CH + u), u, lambda k: True, c)
            for n in range(NBLK, NBLK + CH + 6):
                step(n, n % CH, lambda k, n=n: 0 <= n - k < NBLK, n // CH - 2)

        def wait_uses(eng, s, n, u, k, ring, per, more=0):
            b = n - k
            if isinstance(b, int):
                if b // ring + 1 + more > 0:
                    eng.wait_ge(s[b % ring], per * (b // ring + 1 + more))
            else:
                off = 2 * CH + u - k
                c8 = n - (2 * CH + u)
                eng.wait_ge(s[off % ring], c8 * (per // ring) + per * (off // ring + 1 + more))

        def after(eng, s, value):
            if not isinstance(value, int) or value > 0:
                eng.wait_ge(s, value)

        def grouped(ap):
            return ap.rearrange("p (a g w) -> p a g w", a=16, w=2)

        def windows(ap):
            return ap.rearrange("p (g a w) -> p a g w", a=16, w=2)

        main = nc.Block()
        with main as block:

            @block.sync
            def _(sp):
                sp.dma_start(w_sb[:, :], w_qkv).then_inc(consts_loaded, 16)
                sp.dma_start(wp_sb[:, :], w_proj).then_inc(consts_loaded, 16)
                sp.dma_start(bp_sb[:, :], b_proj.rearrange("(a c) -> a c", a=1).to_broadcast([P, C]))\
                  .then_inc(consts_loaded, 16)
                sp.dma_start(gw_in[:, :], gate_w).then_inc(consts_loaded, 16)
                for h in range(2):
                    sp.dma_start(gb2[64 * h:64 * h + 64, :], gate_b.rearrange("(e a) -> e a", a=1))\
                      .then_inc(consts_loaded, 16)
                for b in range(2):
                    sp.dma_start(xin[b], x_blk[b]).then_inc(x_loaded[b], 16)

                sp.dma_start(b1_in[:, :], weight1[:, C, :]).then_inc(biases_loaded, 16)
                for h in range(2):
                    sp.dma_start(b2_sb[64 * h:64 * h + 64, :], weight2[:, HID, :]).then_inc(biases_loaded, 16)

                sp.wait_ge(zeroed, 5)

                def step(n, u, has, chunk):
                    if has(-2):
                        if has(2):
                            sp.wait_ge(xb_ready, n - 2 + 1)
                        sp.dma_start(xin[(u + 2) % 4], x_blk[bass.ds(n + 2, 1)].rearrange("a p c -> (a p) c"))\
                          .then_inc(x_loaded[(u + 2) % 4], 16)
                    if has(LN2):
                        after(sp, t_ready, n - LN2 + 1)
                        sp.dma_start(out_blk[bass.ds(n - LN2, 1)].rearrange("a p c -> (a p) c"),
                                     xt[(u - LN2) % 8]).then_inc(stored[(u - LN2) % 8], 16)
                    if has(QKV):
                        i = (u - QKV) % 2
                        if has(QKV + 2):
                            sp.wait_ge(scored, n - QKV - 2 + 1)
                        after(sp, kT_ready, n - QKV + 1)
                        for h in range(HEADS):
                            sp.dma_start(kbd[i][32 * h:32 * h + 32, 512 * h:512 * h + 512],
                                         kT[i][32 * h:32 * h + 32, :]).then_inc(kbd_moved[i], 16)
                    if has(PT):
                        i = (u - PT) % 2
                        after(sp, pT_ready, n - PT + 1)
                        for g in range(4):
                            sp.dma_start(pbd[i][32 * g:32 * g + 32, 512 * g:512 * g + 512],
                                         pT[i][32 * g:32 * g + 32, :]).then_inc(pbd_moved[i], 16)

                for n in range(2 * CH):
                    step(n, n % CH, lambda k, n=n: 0 <= n - k < NBLK, None)
                with sp.Fori(0, NCH - 3) as c:
                    for u in range(CH):
                        step(CH * c + (2 * CH + u), u, lambda k: True, None)
                for n in range(NBLK - CH, NBLK + CH):
                    step(n, n % CH, lambda k, n=n: 0 <= n - k < NBLK, None)
                    e = n - (NBLK - CH)
                    sp.dma_start(w1r[:, e, :], weight1[e, 0:C, :]).then_inc(w1_loaded[e], 16)
                    sp.dma_start(w2r[:, e, :], weight2[e, 0:HID, :].rearrange("(p a) o -> p (a o)", a=J))\
                      .then_inc(w2_loaded[e], 16)
                for i in range(8):
                    sp.wait_ge(stored[i], 16 * (NBLK // 8))

            @block.gpsimd
            def _(pool):
                pool.memset(ident[:, :], 0.0).then_inc(ident_zero, 1)
                pool.memset(arena_a[:, 4096:8192], 0.0).then_inc(zeroed, 1)
                pool.memset(arena_b[:, 0:4096], 0.0).then_inc(zeroed, 1)
                pool.memset(eps8[:, 0:4], 1e-6).then_inc(consts_set, 1)
                pool.memset(eps8[:, 4:8], 1e-5).then_inc(consts_set, 1)
                pool.memset(minus_half[:, :], -0.5).then_inc(consts_set, 1)
                pool.wait_ge(ident_zero, 1)
                pool.affine_select(out=ident[:, :], in_=ident[:, :], compare_op=ALU.not_equal, fill=1.0,
                                   base=0, pattern=[[-1, P]], channel_multiplier=1).then_inc(consts_set, 1)
                pool.wait_ge(consts_set, 4)
                pool.wait_ge(consts_loaded, 96)

                def step(n, u, has, chunk):
                    ln1, ln2 = has(0), has(LN2)
                    lo, hi = (0 if ln1 else 4), (8 if ln2 else 4)
                    i = u % 2
                    if has(XT):
                        b = xt[(u - XT) % 8].rearrange("p (j c) -> p j c", j=J)
                        if has(XT + 8):
                            wait_uses(pool, stored, n, u, XT + 8, 8, 16)
                            pool.wait_ge(tn_ready, n - XT - 8 + 1)
                        pool.wait_ge(xn_ready, n - XT + 1)
                        pool.tensor_tensor(b, xin[(u - XT) % 4].rearrange("p (j c) -> p j c", j=J), bp_sb[:, :].unsqueeze(1).to_broadcast([P, J, C]), ALU.add)\
                            .then_inc(xb_ready, 1)
                    if ln1 or ln2:
                        pool.wait_ge(var_ready, n + 1)
                        if has(2):
                            pool.wait_ge(xn_ready, n - 2 + 1)
                        if has(LN2 + 2):
                            pool.wait_ge(tn_ready, n - LN2 - 2 + 1)
                        pool.tensor_tensor(rstd[i][:, lo:hi], vareps[i][:, lo:hi], minus_half[:, lo:hi], ALU.pow)\
                            .then_inc(rstd_ready, 1)
                    if has(SM):
                        k = (u - SM) % 2
                        b = pr[k].rearrange("p (a m) -> p a m", m=32)
                        if ln2:
                            pool.wait_ge(nmr_ready, n + 1)
                            if has(LN2 + 2):
                                pool.wait_ge(t_turned, n - LN2 - 2 + 1)
                        pool.wait_ge(rc_ready, n - SM + 1)
                        pool.tensor_tensor(b, b, rc[k][:, :].unsqueeze(2).to_broadcast([P, G, 32]), ALU.mult)\
                            .then_inc(p_normed, 1)
                    if ln2:
                        t = xt[(u - LN2) % 8]
                        k = (u - LN2) % 2
                        if not has(SM):
                            pool.wait_ge(nmr_ready, n + 1)
                            pool.wait_ge(t_turned, n - LN2 - 2 + 1)
                        for j in range(J):
                            ins = pool.tensor_scalar(tn[k][:, C * j:C * j + C], t[:, C * j:C * j + C],
                                                     rstd[i][:, 4 + j:5 + j], nmr[i][:, 4 + j:5 + j],
                                                     ALU.mult, ALU.add)
                        ins.then_inc(tn_ready, 1)
                slots(pool, step)

            @block.tensor
            def _(pe):
                pe.wait_ge(consts_set, 4)
                pe.wait_ge(consts_loaded, 96)
                pe.transpose(ps_t[:, 0:E], gw_in[:, :], ident[0:E, 0:E]).then_inc(gw_turned, 1)
                pe.wait_ge(gwT_ready, 1)
                pe.wait_ge(biases_loaded, 48)
                for a in range(J):
                    ins = pe.transpose(ps_x[:, E * a:E * a + E], b1_in[:, a::J], ident[0:E, 0:E])
                ins.then_inc(gw_turned, 1)
                pe.wait_ge(gwT_ready, 2)
                pe.wait_ge(zeroed, 5)

                def step(n, u, has, chunk):
                    if has(QKV):
                        i = (u - QKV) % 2
                        pe.wait_ge(xnT_ready, n - QKV + 1)
                        after(pe, kT_ready, n - QKV)
                        pe.matmul(ps_k[:, :], w_sb[:, C:2 * C], xnT[i][:, :], start=True, stop=True)\
                          .then_inc(k_done, 1)
                    if has(XT):
                        pe.wait_ge(xn_ready, n - XT + 1)
                        after(pe, xnT_ready, n - XT)
                        for j in range(J):
                            ins = pe.transpose(ps_x[:, P * j:P * j + P], xn[(u - XT) % 2][:, P * j:P * j + P],
                                               ident[:, :])
                        ins.then_inc(x_turned, 1)
                    if has(QKV):
                        i = (u - QKV) % 2
                        after(pe, qT_ready, n - QKV)
                        pe.matmul(ps_q[:, :], w_sb[:, 0:C], xnT[i][:, :], start=True, stop=True)\
                          .then_inc(q_done, 1)
                    if has(GATE):
                        pe.wait_ge(tn_ready, n - GATE + 1)
                        after(pe, l_ready, n - GATE)
                        for j in range(J):
                            ins = pe.transpose(ps_t[:, P * j:P * j + P], tn[(u - GATE) % 2][:, P * j:P * j + P],
                                               ident[:, :])
                        ins.then_inc(t_turned, 1)
                    if has(PV):
                        i = (u - PV) % 2
                        wait_uses(pe, pbd_moved, n, u, PV, 2, 64)
                        after(pe, oT_ready, n - PV)
                        pb = pbd[i].rearrange("p (g m) -> p g m", g=4)
                        vv = v[(u - PV) % 4]
                        for t in range(J):
                            for h in range(HEADS):
                                m = P * t + HD * h
                                ins = pe.matmul(ps_o[HD * h:HD * h + HD, P * t:P * t + P], vv[:, m:m + HD],
                                                pb[:, :, m:m + 32], start=True, stop=True)
                        ins.then_inc(pv_done, 1)
                    if has(QKV):
                        i = (u - QKV) % 2
                        after(pe, v_ready, n - QKV)
                        for t in range(J):
                            ins = pe.matmul(ps_v[:, P * t:P * t + P], xnT[i][:, P * t:P * t + P],
                                            w_sb[:, 2 * C:3 * C], start=True, stop=True)
                        ins.then_inc(v_done, 1)
                    if has(SC):
                        i = (u - SC) % 2
                        wait_uses(pe, kbd_moved, n, u, SC, 2, 64)
                        pe.wait_ge(qT_ready, n - SC + 1)
                        after(pe, shifted, n - SC)
                        pe.matmul(ps_s[:, :], mask_q[:, :], mask_k[:, :], start=True, stop=False,
                                  skip_group_check=True)
                        kk = kbd[i].rearrange("p (h m) -> p h m", h=HEADS)
                        for t in range(J):
                            for g in range(4):
                                m = 32 * (4 * t + g)
                                ins = pe.matmul(ps_s[32 * g:32 * g + 32, P * t:P * t + P], qT[i][:, m:m + 32],
                                                kk[:, :, m:m + 32], start=False, stop=(t == 3),
                                                skip_group_check=True)
                        ins.then_inc(scored, 1)
                    if has(PV):
                        pe.wait_ge(oT_ready, n - PV + 1)
                        after(pe, t_ready, n - PV)
                        for j in range(J):
                            ins = pe.matmul(ps_y[:, P * j:P * j + P], oT[(u - PV) % 2][:, P * j:P * j + P],
                                            wp_sb[:, :], start=True, stop=True)
                        ins.then_inc(y_done, 1)
                    if has(GATE):
                        pe.wait_ge(tnT_ready, n - GATE + 1)
                        for hf in range(2):
                            ins = pe.matmul(ps_t[64 * hf:64 * hf + 64, 0:256], gwT[:, :],
                                            tnT[(u - GATE) % 2][:, 256 * hf:256 * hf + 256], start=True, stop=True)
                        ins.then_inc(gate_done, 1)

                slots(pe, step)

            @block.scalar
            def _(act):
                act.wait_ge(consts_set, 4)
                nc.scalar.activation(early[:, 0:1], ident[:, 0:1], ACT.Exp).then_inc(exp_primed, 1)
                act.wait_ge(exp_primed, 1)
                act.sem_inc(chunk_summed, 1)
                act.wait_ge(gw_turned, 1)
                nc.scalar.activation(gwT[:, :], ps_t[:, 0:E], ACT.Copy).then_inc(gwT_ready, 1)
                act.wait_ge(gw_turned, 2)
                nc.scalar.activation(b1T[:, :, :], ps_x[:, 0:J * E].rearrange("p (a e) -> p a e", a=J), ACT.Copy)\
                    .then_inc(gwT_ready, 1)
                act.wait_ge(gwT_ready, 2)

                def step(n, u, has, chunk):
                    if has(GATE + 1):
                        k = (u - GATE - 1) % CH
                        if k == 0 and chunk is not None:
                            act.wait_ge(early_copied, chunk + 1)
                        if k == 4 and chunk is not None:
                            act.wait_ge(chunk_summed, chunk + 2)
                        act.wait_ge(gate_done, n - GATE - 1 + 1)
                        place = early if k < 4 else logits
                        nc.scalar.activation(place[:, 256 * k:256 * k + 256], ps_t[:, 0:256], ACT.Identity,
                                             bias=gb2[:, 0:1]).then_inc(l_ready, 1)
                    if has(QKV):
                        i = (u - QKV) % 2
                        act.wait_ge(k_done, n - QKV + 1)
                        if has(QKV + 2):
                            wait_uses(act, kbd_moved, n, u, QKV + 2, 2, 64)
                        nc.scalar.activation(kT[i], ps_k[:, :], ACT.Copy).then_inc(kT_ready, 1)
                    if has(XT):
                        act.wait_ge(x_turned, n - XT + 1)
                        if has(XT + 2):
                            act.wait_ge(v_done, n - XT - 2 + 1)
                        nc.scalar.activation(windows(xnT[(u - XT) % 2]), grouped(ps_x[:, :]), ACT.Copy)\
                            .then_inc(xnT_ready, 1)
                    if has(SM):
                        act.wait_ge(shifted, n - SM + 1)
                        b = pr[(u - SM) % 2]
                        nc.scalar.activation(b, b, ACT.Exp, scale=SCALE).then_inc(exp_done, 1)
                    if has(QKV):
                        i = (u - QKV) % 2
                        act.wait_ge(q_done, n - QKV + 1)
                        if has(QKV + 2):
                            act.wait_ge(scored, n - QKV - 2 + 1)
                        nc.scalar.activation(qT[i], ps_q[:, :], ACT.Copy).then_inc(qT_ready, 1)
                    if has(GATE):
                        act.wait_ge(t_turned, n - GATE + 1)
                        if has(GATE + 2):
                            act.wait_ge(gate_done, n - GATE - 2 + 1)
                        nc.scalar.activation(
                            tnT[(u - GATE) % 2][:, :].rearrange("c (f p a) -> c a f p", f=2, a=2),
                            ps_t[:, :].rearrange("c (a f p) -> c a f p", a=2, f=2), ACT.Copy).then_inc(tnT_ready, 1)
                    if has(PV):
                        act.wait_ge(pv_done, n - PV + 1)
                        if has(PV + 2):
                            act.wait_ge(y_done, n - PV - 2 + 1)
                        nc.scalar.activation(grouped(oT[(u - PV) % 2][:, :]), windows(ps_o[:, :]), ACT.Copy)\
                            .then_inc(oT_ready, 1)
                    if has(QKV):
                        act.wait_ge(v_done, n - QKV + 1)
                        if has(QKV + 4):
                            act.wait_ge(pv_done, n - QKV - 4 + 1)
                        nc.scalar.activation(v[(u - QKV) % 4], ps_v[:, :], ACT.Copy).then_inc(v_ready, 1)
                    if has(0):
                        i = u % 2
                        act.wait_ge(nmr_ready, n + 1)
                        if has(2):
                            act.wait_ge(x_turned, n - 2 + 1)
                        for j in range(J):
                            ins = nc.scalar.activation(xn[i][:, C * j:C * j + C], xin[u % 4][:, C * j:C * j + C],
                                                       ACT.Identity, bias=nmr[i][:, j:j + 1],
                                                       scale=rstd[i][:, j:j + 1])
                        ins.then_inc(xn_ready, 1)
                    if u == 7 and has(GATE + 6):
                        act.wait_ge(l_ready, n - GATE - 3 + 1)
                        if chunk is not None:
                            act.wait_ge(chunk_summed, chunk + 2)
                        nc.scalar.activation(logits[:, 0:1024], early[:, :], ACT.Copy).then_inc(early_copied, 1)
                    if u == 5 and chunk is not None:
                        act.wait_ge(negm_ready, chunk + 1)
                        act.wait_ge(chunk_kept, chunk + 2)
                        act.wait_ge(chunk_summed, chunk + 1)
                        nc.scalar.activation(logits[:, :], logits[:, :], ACT.Exp, bias=negm[:, 0:1],
                                             accum_out=sums[:, bass.ds(chunk, 1)]).then_inc(chunk_summed, 1)

                slots(act, step)

            @block.vector
            def _(dve):
                dve.memset(mask_q[:, :].bitcast(U32), 0).then_inc(mask_zero, 1)
                dve.memset(mask_k[:, :].bitcast(U32), 0).then_inc(mask_zero, 1)
                dve.wait_ge(mask_zero, 2)
                for row in range(2):
                    dve.memset(mask_q[32 * row:32 * row + 1, row::2], 1.0).then_inc(zeroed, 1)
                dve.memset(mask_k[0:1, 1::2], MASKED)
                dve.memset(mask_k[32:33, 0::2], MASKED).then_inc(zeroed, 1)
                dve.memset(half[0:64, :], 0.0)
                dve.memset(half[64:128, :], 1.0).then_inc(half_set, 1)
                dve.wait_ge(half_set, 1)
                dve.sem_inc(chunk_kept, 1)
                dve.wait_ge(consts_set, 4)

                def step(n, u, has, chunk):
                    i = u % 2
                    ln1, ln2 = has(0), has(LN2)
                    lo, hi = (0 if ln1 else 4), (8 if ln2 else 4)
                    if has(SM):
                        k = (u - SM) % 2
                        s16 = ps_s[:, :].rearrange("p (a m) -> p a m", m=32)
                        dve.wait_ge(scored, n - SM + 1)
                        dve.tensor_reduce(mx[k][:, :], s16, X, ALU.max).then_inc(mx_ready, 1)
                        dve.wait_ge(mx_ready, n - SM + 1)
                        if has(SM + 2):
                            dve.wait_ge(pT_ready, n - SM - 2 + 1)
                        dve.tensor_tensor(pr[k].rearrange("p (a m) -> p a m", m=32), s16,
                                          mx[k][:, :].unsqueeze(2).to_broadcast([P, G, 32]), ALU.subtract)\
                           .then_inc(shifted, 1)
                    if ln1 or ln2:
                        after(dve, cvar_ready, n)
                        if ln2:
                            dve.wait_ge(t_ready, n - LN2 + 1)
                            for j in range(J):
                                ins = dve.bn_stats(raw[i][:, 4 + j, :], xt[(u - LN2) % 8][:, C * j:C * j + C])
                        if ln1:
                            wait_uses(dve, x_loaded, n, u, 0, 4, 16)
                            for j in range(J):
                                ins = dve.bn_stats(raw[i][:, j, :], xin[u % 4][:, C * j:C * j + C])
                        ins.then_inc(raw_ready, 1)
                        dve.wait_ge(raw_ready, n + 1)
                        r = raw[i]
                        after(dve, nmr_ready, n - 1)
                        dve.tensor_tensor(mean2[i][:, lo:hi], r[:, lo:hi, 1], r[:, lo:hi, 4], ALU.add)
                        dve.tensor_tensor(mdiff[:, lo:hi], r[:, lo:hi, 1], r[:, lo:hi, 4], ALU.subtract)\
                           .then_inc(mdiff_ready, 1)
                        dve.tensor_tensor(csum[:, lo:hi], r[:, lo:hi, 2], r[:, lo:hi, 5], ALU.add)\
                           .then_inc(csum_ready, 1)
                        dve.wait_ge(mdiff_ready, n + 1)
                        dve.scalar_tensor_tensor(out=mdiff2[:, lo:hi], in0=mdiff[:, lo:hi], scalar=C / 4.0,
                                                 in1=mdiff[:, lo:hi], op0=ALU.mult, op1=ALU.mult)\
                           .then_inc(mdiff2_ready, 1)
                        dve.wait_ge(csum_ready, n + 1)
                        dve.wait_ge(mdiff2_ready, n + 1)
                        dve.tensor_tensor(cvar[:, lo:hi], mdiff2[:, lo:hi], csum[:, lo:hi], ALU.add)\
                           .then_inc(cvar_ready, 1)
                        dve.wait_ge(cvar_ready, n + 1)
                        after(dve, rstd_ready, n - 1)
                        dve.scalar_tensor_tensor(out=vareps[i][:, lo:hi], in0=cvar[:, lo:hi], scalar=1.0 / C,
                                                 in1=eps8[:, lo:hi], op0=ALU.mult, op1=ALU.add)\
                           .then_inc(var_ready, 1)
                    if has(ADD):
                        dve.wait_ge(xb_ready, n - ADD + 1)
                        dve.wait_ge(y_done, n - ADD + 1)
                        b = xt[(u - ADD) % 8]
                        dve.tensor_tensor(b, ps_y[:, :], b, ALU.add).then_inc(t_ready, 1)
                    if has(PT):
                        k = (u - PT) % 2
                        dve.wait_ge(p_normed, n - PT + 1)
                        if has(PT + 2):
                            wait_uses(dve, pbd_moved, n, u, PT + 2, 2, 64)
                            dve.wait_ge(pv_done, n - PT - 2 + 1)
                        dve.transpose(pT[k], pr[k]).then_inc(pT_ready, 1)
                    if has(SM):
                        k = (u - SM) % 2
                        dve.wait_ge(exp_done, n - SM + 1)
                        dve.tensor_reduce(sm[k][:, :], pr[k].rearrange("p (a m) -> p a m", m=32), X, ALU.add)\
                           .then_inc(sm_ready, 1)
                        dve.wait_ge(sm_ready, n - SM + 1)
                        if has(SM + 2):
                            dve.wait_ge(p_normed, n - SM - 2 + 1)
                        dve.reciprocal(rc[k][:, :], sm[k][:, :]).then_inc(rc_ready, 1)
                    if u == 1 and chunk is not None:
                        dve.wait_ge(l_ready, CH * chunk + CH)
                        dve.wait_ge(early_copied, chunk + 1)
                        dve.wait_ge(chunk_kept, chunk + 1)
                    if ln1 or ln2:
                        dve.wait_ge(rstd_ready, n + 1)
                        if has(2):
                            dve.wait_ge(xn_ready, n - 2 + 1)
                        if has(LN2 + 2):
                            dve.wait_ge(tn_ready, n - LN2 - 2 + 1)
                        dve.scalar_tensor_tensor(out=nmr[i][:, lo:hi], in0=mean2[i][:, lo:hi], scalar=-0.5,
                                                 in1=rstd[i][:, lo:hi], op0=ALU.mult, op1=ALU.mult)\
                           .then_inc(nmr_ready, 1)
                    if u == 1 and chunk is not None:
                        dve.max(v8[:, :], logits[:, :]).then_inc(v8_ready, 1)
                    if u == 4 and chunk is not None:
                        dve.wait_ge(v8_ready, chunk + 1)
                        dve.wait_ge(chunk_summed, chunk + 1)
                        dve.tensor_scalar(negm[:, :], v8[:, 0:1], -1.0, None, ALU.mult).then_inc(negm_ready, 1)
                        dve.max_index(i8[:, :], v8[:, :], logits[:, :]).then_inc(i8_ready, 1)
                        dve.tensor_copy(vals[:, bass.ds(8 * chunk, 8)], v8[:, :])
                        dve.wait_ge(i8_ready, chunk + 1)
                        dve.tensor_scalar(toks[:, bass.ds(8 * chunk, 8)], i8[:, :], 2.0, half[:, 0:1],
                                          ALU.mult, ALU.add).then_inc(chunk_kept, 1)

                slots(dve, step)

        cand_v, cand_t = (arena_d[:, 512 * i:512 * i + 512].rearrange("p (b f m) -> p b f m", b=PAIRS, f=2)
                          for i in range(2))
        cand_s = sb("cand_s", [P, PAIRS, 2, 4])
        chunk_base = arena_b[:, 0:NCH * K8].rearrange("p (c k) -> p c k", k=K8)
        iota64 = sb("iota64", [P, 64])
        earlier = arena_d[:, 1024:2048]
        top_m = sb("top_m", [P, PAIRS])
        rel_m = sb("rel_m", [P, PAIRS, 8])
        den = sb("den", [P, PAIRS])
        rden = sb("rden", [P, PAIRS])
        top_v = sb("top_v", [P, PAIRS, K8])
        top_i = sb("top_i", [P, PAIRS, K8], U32)
        top_f = sb("top_f", [P, 64])
        top_p = sb("top_p", [P, 64])
        tokf = sb("tokf", [P, 64])
        toku = sb("toku", [P, 64], U32)
        twice = sb("twice", [P, 64])
        put_f = sb("put_f", [P, 64])
        put_u = sb("put_u", [P, 64], U32)
        g_raw = sb("g_raw", [P, 64, 6])
        g_mv = sb("g_mv", [P, 64, 2])
        g_var = sb("g_var", [P, 64])
        g_rstd = sb("g_rstd", [P, 64])
        g_coef = sb("g_coef", [P, 64])
        g_mean = sb("g_mean", [P, 64])
        g_off = sb("g_off", [P, PAIRS])
        pooled = tn[0], tn[1]
        pooledT = arena_c[:, 1024:2048].rearrange("p (b r e) -> p b r e", r=2, e=E)
        hid = oT
        rows_out = tnT
        tok_rows = logits[:, 0:1024]
        hits = logits[:, 1024:2048]
        outs = [arena_c[:, 2048 + 512 * i:2560 + 512 * i].rearrange("p (a o) -> p a o", a=J) for i in range(2)]
        expert_out = arena_c[:, 0:1024].rearrange("p (b c) -> p b c", c=C)
        spare = sb("spare", [P, 1])

        tail_consts = sem("tail_consts")
        based = sem("based")
        cands_moved = sem("cands_moved")
        d_step = sem("d_step")
        m_shift = sem("m_shift")
        m_exp = sem("m_exp")
        v_shift = sem("v_shift")
        v_exp = sem("v_exp")
        toku_ready = sem("toku_ready")
        gathers_in = sem("gathers_in")
        g_var_ready = sem("g_var_ready")
        g_rstd_ready = sem("g_rstd_ready")
        pooled_ready = sem("pooled_ready")
        pooled_turned = sem("pooled_turned")
        pooledT_ready = sem("pooledT_ready")
        h_done = sem("h_done")
        h_biased = sem("h_biased")
        h_ready = sem("h_ready")
        o_done = sem("o_done")
        o_copied = sem("o_copied")
        o_stored = [sem(f"o_stored{i}") for i in range(2)]
        eo_loaded = sem("eo_loaded")
        eo_ready = sem("eo_ready")
        tokr_done = sem("tokr_done")
        tokr_copied = sem("tokr_copied")
        tokr_used = sem("tokr_used")
        wsel_ready = sem("wsel_ready")
        put_ready = sem("put_ready")
        rows_done = sem("rows_done")
        rows_added = sem("rows_added")
        rows_put = sem("rows_put")

        ps_h, ps_e, ps_r, ps_w = bank[0:2], bank[2:4], bank[4:6], bank[6:8]
        cv64 = cand_v[:, :, :, :].rearrange("p b f m -> p b (f m)")
        ct64 = cand_t[:, :, :, :].rearrange("p b f m -> p b (f m)")
        cs8 = cand_s[:, :, :, :].rearrange("p b f q -> p b (f q)")
        cm8 = cand_v[:, :, :, :].rearrange("p b f (q k) -> p b (f q) k", k=K8)[:, :, :, 0]

        with nc.Block() as block:

            @block.sync
            def _(sp):
                sp.wait_ge(based, 1)
                for par in range(2):
                    for hf in range(2):
                        d, s = slice(64 * par, 64 * par + 64), slice(64 * hf, 64 * hf + 64)
                        sp.dma_start(cand_v[d, :, hf, :],
                                     vals[s, :].rearrange("p (b r m) -> p b r m", r=2, m=4 * K8)[:, :, par, :])\
                          .then_inc(cands_moved, 16)
                        sp.dma_start(cand_t[d, :, hf, :],
                                     toks[s, :].rearrange("p (b r m) -> p b r m", r=2, m=4 * K8)[:, :, par, :])\
                          .then_inc(cands_moved, 16)
                        sp.dma_start(cand_s[d, :, hf, :],
                                     sums[s, :].rearrange("p (b r m) -> p b r m", r=2, m=4)[:, :, par, :])\
                          .then_inc(cands_moved, 16)
                for e in range(RING, E):
                    sp.wait_ge(o_done, (e - RING) // 8 + 1)
                    sp.dma_start(w1r[:, e % RING, :], weight1[e, 0:C, :]).then_inc(w1_loaded[e % RING], 16)
                    sp.dma_start(w2r[:, e % RING, :], weight2[e, 0:HID, :].rearrange("(p a) o -> p (a o)", a=J))\
                      .then_inc(w2_loaded[e % RING], 16)
                for i in range(2):
                    sp.wait_ge(o_stored[i], 128)
                for par in range(2):
                    sp.dma_start(expert_out[64 * par:64 * par + 64, :, :],
                                 expert_dram.rearrange("(b r) e o -> r e b o", r=2)[par])\
                      .then_inc(eo_loaded, 16)

            @block.gpsimd
            def _(pool):
                pool.iota(chunk_base[:, :, :], pattern=[[2 * 256 * CH, NCH], [0, K8]], base=0, channel_multiplier=0,
                          allow_small_or_imprecise_dtypes=True).then_inc(tail_consts, 1)
                pool.iota(iota64[:, :], pattern=[[1, 64]], base=0, channel_multiplier=0,
                          allow_small_or_imprecise_dtypes=True).then_inc(tail_consts, 1)
                pool.memset(earlier[:, :], 1.0).then_inc(tail_consts, 1)
                pool.wait_ge(tail_consts, 3)
                last = earlier[:, (K8 - 1) * P:]
                pool.affine_select(out=last, in_=last, compare_op=ALU.is_gt, fill=0.0, base=0,
                                   pattern=[[-1, P]], channel_multiplier=1).then_inc(tail_consts, 1)
                pool.wait_ge(toku_ready, 1)
                for n in range(64):
                    pool.indirect_dma_start(gathered[:, n, :], None, out_rows,
                                            bass.IndirectOffsetOnAxis(ap=toku[:, n:n + 1], axis=0))\
                        .then_inc(gathers_in, 16)
                pool.wait_ge(g_var_ready, 1)
                pool.tensor_tensor(g_rstd[:, :], g_var[:, :], minus_half[:, :], ALU.pow).then_inc(g_rstd_ready, 1)
                for b in range(PAIRS):
                    for q in range(2):
                        pool.wait_ge(rows_added, 2 * b + q + 1)
                        if b == 0 and q == 0:
                            pool.wait_ge(put_ready, 1)
                        for k in range(4):
                            n = K8 * b + 4 * q + k
                            pool.indirect_dma_start(out_rows, bass.IndirectOffsetOnAxis(ap=put_u[:, n:n + 1], axis=0),
                                                    gathered[:, n, :], None, bounds_check=B * S - 1,
                                                    oob_is_err=False).then_inc(rows_put, 16)
                pool.wait_ge(rows_put, 64 * 16)

            @block.vector
            def _(dve):
                count = [0]

                def keep(ins):
                    count[0] += 1
                    ins.then_inc(d_step, 1)

                def kept():
                    dve.wait_ge(d_step, count[0])

                dve.wait_ge(tail_consts, 4)
                t3 = toks[:, :].rearrange("p (c k) -> p c k", k=K8)
                dve.tensor_tensor(t3, t3, chunk_base[:, :, :], ALU.add).then_inc(based, 1)
                dve.wait_ge(cands_moved, 12 * 16)
                keep(dve.tensor_reduce(top_m[:, :], cv64, X, ALU.max))
                kept()
                dve.tensor_tensor(rel_m[:, :, :], cm8, top_m[:, :].unsqueeze(2).to_broadcast([P, PAIRS, 8]),
                                  ALU.subtract).then_inc(m_shift, 1)
                for b in range(PAIRS):
                    ins = dve.max(top_v[:, b, :], cv64[:, b, :])
                keep(ins)
                kept()
                for b in range(PAIRS):
                    ins = dve.max_index(top_i[:, b, :], top_v[:, b, :], cv64[:, b, :])
                keep(ins)
                kept()
                keep(dve.tensor_copy(top_f[:, :], top_i[:, :, :].rearrange("p b k -> p (b k)")))
                kept()
                keep(dve.tensor_tensor(onehot, iota64[:, :].unsqueeze(1).to_broadcast([P, 64, 64]),
                                       top_f[:, :].unsqueeze(2).to_broadcast([P, 64, 64]), ALU.is_equal))
                kept()
                for b in range(PAIRS):
                    o = onehot[:, K8 * b:K8 * b + K8, :]
                    ins = dve.tensor_tensor(o, o, ct64[:, b, :].unsqueeze(1).to_broadcast([P, K8, 64]), ALU.mult)
                keep(ins)
                kept()
                keep(dve.tensor_reduce(tokf[:, :], onehot, X, ALU.add))
                kept()
                dve.tensor_copy(toku[:, :], tokf[:, :]).then_inc(toku_ready, 1)
                tv = top_v[:, :, :]
                dve.tensor_tensor(top_p[:, :].rearrange("p (b k) -> p b k", k=K8), tv,
                                  top_m[:, :].unsqueeze(2).to_broadcast([P, PAIRS, K8]), ALU.subtract)\
                   .then_inc(v_shift, 1)
                dve.wait_ge(m_exp, 1)
                keep(dve.tensor_tensor(rel_m[:, :, :], rel_m[:, :, :], cs8, ALU.mult))
                kept()
                keep(dve.tensor_reduce(den[:, :], rel_m[:, :, :], X, ALU.add))
                kept()
                keep(dve.reciprocal(rden[:, :], den[:, :]))
                kept()
                dve.wait_ge(v_exp, 1)
                tp = top_p[:, :].rearrange("p (b k) -> p b k", k=K8)
                keep(dve.tensor_tensor(tp, tp, rden[:, :].unsqueeze(2).to_broadcast([P, PAIRS, K8]), ALU.mult))
                kept()
                dve.wait_ge(gathers_in, 64 * 16)
                for n in range(64):
                    ins = dve.bn_stats(g_raw[:, n, :], gathered[:, n, :])
                keep(ins)
                kept()
                for n in range(64):
                    ins = dve.bn_aggr(g_mv[:, n, :], g_raw[:, n, :])
                keep(ins)
                kept()
                dve.tensor_scalar(g_var[:, :], g_mv[:, :, 1], 1e-5, None, ALU.add).then_inc(g_var_ready, 1)
                dve.wait_ge(g_rstd_ready, 1)
                keep(dve.tensor_tensor(g_coef[:, :], g_rstd[:, :], top_p[:, :], ALU.mult))
                kept()
                keep(dve.scalar_tensor_tensor(out=g_mean[:, :], in0=g_mv[:, :, 0], scalar=-1.0, in1=g_coef[:, :],
                                              op0=ALU.mult, op1=ALU.mult))
                kept()
                keep(dve.tensor_reduce(g_off[:, :], g_mean[:, :].rearrange("p (b k) -> p b k", k=K8), X, ALU.add))
                kept()
                for k in range(K8):
                    for b in range(PAIRS):
                        n = K8 * b + k
                        dst = pooled[b // 4][:, C * (b % 4):C * (b % 4) + C]
                        if k == 0:
                            ins = dve.tensor_scalar(dst, gathered[:, n, :], g_coef[:, n:n + 1], g_off[:, b:b + 1],
                                                    ALU.mult, ALU.add)
                        else:
                            ins = dve.scalar_tensor_tensor(out=dst, in0=gathered[:, n, :], scalar=g_coef[:, n:n + 1],
                                                           in1=dst, op0=ALU.mult, op1=ALU.add)
                    if k < K8 - 1:
                        keep(ins)
                        kept()
                ins.then_inc(pooled_ready, 1)

                def bias_hidden(g):
                    dve.wait_ge(h_done, g + 1)
                    if g >= 2:
                        dve.wait_ge(o_done, g - 1)
                    dve.tensor_tensor(
                        hid[g % 2][:, :].rearrange("p (e a b) -> p e a b", e=8, a=J),
                        ps_h[g % 2][:, :].rearrange("p (e a b) -> p e a b", e=8, a=J),
                        b1T[:, :, 8 * g:8 * g + 8].rearrange("p a e -> p e a").unsqueeze(3)
                        .to_broadcast([P, 8, J, B]), ALU.add).then_inc(h_biased, 1)

                def select(b):
                    dve.wait_ge(tokr_copied, b + 1)
                    for k in range(K8):
                        n = K8 * b + k
                        dst = wsel[:, b, :] if k == 0 else hits
                        keep(dve.tensor_scalar(dst, tok_rows, tokf[:, n:n + 1], top_p[:, n:n + 1],
                                               ALU.is_equal, ALU.mult))
                        if k:
                            kept()
                            keep(dve.tensor_tensor(wsel[:, b, :], wsel[:, b, :], hits, ALU.add))
                            kept()
                    for k in range(K8):
                        n = K8 * b + k
                        m = P * (k + 1)
                        ins = dve.scalar_tensor_tensor(out=hits[:, 0:m], in0=tok_rows[:, 0:m], scalar=tokf[:, n:n + 1],
                                                       in1=earlier[:, P * K8 - m:], op0=ALU.is_equal, op1=ALU.mult,
                                                       accum_out=twice[:, n:n + 1])
                        keep(ins)
                        kept()
                    dve.tensor_copy(spare[:, :], tokf[:, 0:1]).then_inc(tokr_used, 1)

                for g in range(NE):
                    bias_hidden(g)
                    select(g)
                keep(dve.scalar_tensor_tensor(out=put_f[:, :], in0=twice[:, :], scalar=float(2 * B * S),
                                              in1=tokf[:, :], op0=ALU.mult, op1=ALU.add))
                kept()
                dve.tensor_copy(put_u[:, :], put_f[:, :]).then_inc(put_ready, 1)
                dve.wait_ge(eo_loaded, 32)
                dve.tensor_tensor(expert_out[:, :, :], expert_out[:, :, :],
                                  b2_sb[:, :].unsqueeze(1).to_broadcast([P, PAIRS, C]), ALU.add)\
                   .then_inc(eo_ready, 1)
                for b in range(PAIRS):
                    for q in range(2):
                        n = K8 * b + 4 * q
                        dve.wait_ge(rows_done, 2 * b + q + 1)
                        rows = gathered[:, n:n + 4, :].rearrange("p n c -> p (n c)")
                        dve.tensor_tensor(rows, ps_r[q][:, :], rows, ALU.add).then_inc(rows_added, 1)

            @block.scalar
            def _(act):
                act.wait_ge(m_shift, 1)
                nc.scalar.activation(rel_m[:, :, :], rel_m[:, :, :], ACT.Exp).then_inc(m_exp, 1)
                act.wait_ge(v_shift, 1)
                nc.scalar.activation(top_p[:, :], top_p[:, :], ACT.Exp).then_inc(v_exp, 1)
                for q in range(2):
                    act.wait_ge(pooled_turned, q + 1)
                    nc.scalar.activation(pooledT[:, 4 * q:4 * q + 4, :, :].rearrange("p b r e -> p (b r e)"),
                                         ps_e[q][:, :], ACT.Copy).then_inc(pooledT_ready, 1)

                def rows_of_tokens(b):
                    if b:
                        act.wait_ge(tokr_used, b)
                    for q in range(2):
                        act.wait_ge(tokr_done, 2 * b + q + 1)
                        ins = nc.scalar.activation(tok_rows[:, 512 * q:512 * q + 512], ps_w[q][:, :], ACT.Copy)
                    ins.then_inc(tokr_copied, 1)

                for g in range(NE):
                    rows_of_tokens(g)
                    act.wait_ge(h_biased, g + 1)
                    nc.scalar.activation(hid[g % 2][:, :], hid[g % 2][:, :], ACT.Gelu).then_inc(h_ready, 1)
                    if g % 2:
                        big = g // 2
                        act.wait_ge(o_done, g + 1)
                        if big >= 2:
                            act.wait_ge(o_stored[big % 2], 64)
                        for q in range(4):
                            nc.scalar.activation(outs[big % 2][32 * q:32 * q + B, :, :].rearrange("p a o -> p (a o)"),
                                                 ps_e[big % 2][32 * q:32 * q + B, :], ACT.Copy).then_inc(o_copied, 1)
                        act.wait_ge(o_copied, 4 * (big + 1))
                        for q in range(4):
                            act.dma_start(expert_dram[:, 16 * big + q:16 * big + 16:4, :],
                                          outs[big % 2][32 * q:32 * q + B, :, :]).then_inc(o_stored[big % 2], 16)

            @block.tensor
            def _(pe):
                pe.wait_ge(toku_ready, 1)

                def rows_of_tokens(b):
                    for q in range(2):
                        if b:
                            pe.wait_ge(tokr_copied, b)
                        for k in range(4):
                            n = K8 * b + 4 * q + k
                            ins = pe.matmul(ps_w[q][:, P * k:P * k + P], tokf[:, n:n + 1].to_broadcast([P, P]),
                                            ident[:, :], start=True, stop=True)
                        ins.then_inc(tokr_done, 1)

                def hidden(g):
                    if g >= 2:
                        pe.wait_ge(h_biased, g - 1)
                    for m in range(8):
                        e = 8 * g + m
                        pe.wait_ge(w1_loaded[e % RING], 16 * (e // RING + 1))
                        for a in range(J):
                            ins = pe.matmul(ps_h[g % 2][:, (J * m + a) * B:(J * m + a + 1) * B],
                                            w1r[:, e % RING, a::J],
                                            pooledT[:, :, :, e], start=True, stop=True)
                    ins.then_inc(h_done, 1)

                def expert_rows(g):
                    pe.wait_ge(h_ready, g + 1)
                    big = g // 2
                    if g % 2 == 0 and big >= 2:
                        pe.wait_ge(o_copied, 4 * (big - 1))
                    for m in range(8):
                        e = 8 * g + m
                        pe.wait_ge(w2_loaded[e % RING], 16 * (e // RING + 1))
                        q, col = e % 4, (e % 16) // 4
                        for a in range(J):
                            ins = pe.matmul(ps_e[big % 2][32 * q:32 * q + B, C * col:C * col + C],
                                            hid[g % 2][:, (J * m + a) * B:(J * m + a + 1) * B],
                                            w2r[:, e % RING, C * a:C * a + C], start=(a == 0), stop=(a == J - 1))
                    ins.then_inc(o_done, 1)

                rows_of_tokens(0)
                pe.wait_ge(pooled_ready, 1)
                for q in range(2):
                    for b in range(4):
                        ins = pe.transpose(ps_e[q][:, P * b:P * b + P], pooled[q][:, C * b:C * b + C], ident[:, :])
                    ins.then_inc(pooled_turned, 1)
                pe.wait_ge(pooledT_ready, 2)
                hidden(0)
                for g in range(NE):
                    if g + 1 < NE:
                        rows_of_tokens(g + 1)
                        hidden(g + 1)
                    expert_rows(g)
                pe.wait_ge(put_ready, 1)
                pe.wait_ge(eo_ready, 1)
                for b in range(PAIRS):
                    for q in range(2):
                        if b:
                            pe.wait_ge(rows_added, 2 * (b - 1) + q + 1)
                        for k in range(4):
                            ins = pe.matmul(ps_r[q][:, C * k:C * k + C],
                                            wsel[:, b, P * (4 * q + k):P * (4 * q + k) + P],
                                            expert_out[:, b, :], start=True, stop=True)
                        ins.then_inc(rows_done, 1)


_INS = ["x", "L0_conv_w_qkv", "L0_conv_w_proj", "L0_conv_b_proj", "L0_ffn_gate_w", "L0_ffn_gate_b",
        "L0_ffn_weight1", "L0_ffn_weight2"]


def kernel(**inputs):
    import numpy as _np
    import concourse.bacc as _bacc
    from concourse.bass_utils import run_bass_kernel_spmd as _run

    nc = _bacc.Bacc("TRN2", target_bir_lowering=False, num_devices=1)
    arrays, args = {}, []
    for name in _INS:
        a = _np.ascontiguousarray(inputs[name])
        arrays[f"in_{name}"] = a
        args.append(nc.dram_tensor(f"in_{name}", a.shape, mybir.dt.from_np(a.dtype), kind="ExternalInput").ap())
    args.append(nc.dram_tensor("out_0", inputs["x"].shape, F32, kind="ExternalOutput").ap())
    metaformer_layer(nc, *args)
    r = _run(nc, [arrays], core_ids=[0])
    return r.results[0]["out_0"]
```

```python
from contextlib import ExitStack

import concourse.bass as bass
from concourse import mybir

F32 = mybir.dt.float32
BF16 = mybir.dt.bfloat16
U32 = mybir.dt.uint32
ALU = mybir.AluOpType
ACT = mybir.ActivationFunctionType
X = mybir.AxisListType.X

P = 128
MASKED = -1e30
XT, QKV, SC, SM, PT, PV, ADD, LN2, GATE = 1, 2, 3, 4, 5, 6, 7, 8, 9


def metaformer_layer(nc, x, w_qkv, w_proj, b_proj, gate_w, gate_b, weight1, weight2, out):
    B, HH, WW, C = x.shape
    E, _, HID = weight1.shape
    HEADS = 4
    HD = C // HEADS
    J = 4
    BT = P * J
    S = HH * WW
    NBLK = B * S // BT
    CH = 8
    NCH = NBLK // CH
    QCH = NCH // B
    G = BT // 32
    K8 = 8
    KEPT = 2 * K8 + 2
    PAIRS = B // 2
    NE = E // 8
    RING = 16
    SCALE = float(HD) ** -0.5
    assert C == P and E == 64 and HID == 4 * P and BT == 4 * WW and NBLK == CH * NCH

    x_blk = x.rearrange("b h w c -> (b h w) c").rearrange("(n p j) c -> n p (j c)", p=P, j=J)
    out_rows = out.rearrange("b h w c -> (b h w) c")
    out_blk = out_rows.rearrange("(n p j) c -> n p (j c)", p=P, j=J)
    expert_dram = nc.dram_tensor("expert_rows", (B, E, C), F32, kind="Internal").ap()

    ctx = ExitStack()
    with ctx:
        def sb(name, shape, dt=F32):
            return ctx.enter_context(nc.sbuf_tensor(name, shape, dt))

        def sem(name):
            return ctx.enter_context(nc.semaphore(name))

        arena_a = sb("arena_a", [P, 8192])
        arena_b = sb("arena_b", [P, 8192])
        arena_c = sb("arena_c", [P, 4096])
        arena_d = sb("arena_d", [P, 2176])
        xin = [arena_d[:, 512 * i:512 * i + 512] for i in range(4)]
        xt = [arena_a[:, 512 * i:512 * i + 512] for i in range(8)]
        kbd = [arena_a[:, 4096 + 2048 * i:6144 + 2048 * i] for i in range(2)]
        pbd = [arena_b[:, 2048 * i:2048 * i + 2048] for i in range(2)]
        xn = [arena_b[:, 4096 + 512 * i:4608 + 512 * i] for i in range(2)]
        xnT = [arena_b[:, 5120 + 512 * i:5632 + 512 * i] for i in range(2)]
        qT = [arena_b[:, 6144 + 512 * i:6656 + 512 * i] for i in range(2)]
        kT = [arena_b[:, 7168 + 512 * i:7680 + 512 * i] for i in range(2)]
        v = [arena_c[:, 512 * i:512 * i + 512] for i in range(4)]
        pr = [arena_c[:, 2048 + 512 * i:2560 + 512 * i] for i in range(2)]
        pT = [arena_c[:, 3072 + 512 * i:3584 + 512 * i] for i in range(2)]
        gathered = arena_a[:, :].rearrange("p (n c) -> p n c", c=C)
        wsel = arena_b[:, :].rearrange("p (b n) -> p b n", b=PAIRS)
        onehot = arena_c[:, :].rearrange("p (n m) -> p n m", m=64)

        oT = [sb(f"oT{i}", [P, 512]) for i in range(2)]
        tn = [sb(f"tn{i}", [P, 512]) for i in range(2)]
        tnT = [sb(f"tnT{i}", [P, 512]) for i in range(2)]
        logits = sb("logits", [P, CH * 256])
        early = sb("early", [P, 1024])
        w_sb = sb("w_sb", [P, 3 * C])
        wp_sb = sb("wp_sb", [P, C])
        bp_sb = sb("bp_sb", [P, C])
        gw_in = sb("gw_in", [E, C])
        gwT = sb("gwT", [P, E])
        gb2 = sb("gb2", [P, 1])
        ident = sb("ident", [P, P])
        mask_q = sb("mask_q", [P, P], BF16)
        mask_k = sb("mask_k", [P, 512], BF16)
        eps8 = sb("eps8", [P, 8])
        minus_half = sb("minus_half", [P, 64])
        base = sb("base", [P, 1])
        raw = [sb(f"raw{i}", [P, 8, 6]) for i in range(2)]
        mean2 = [sb(f"mean2{i}", [P, 8]) for i in range(2)]
        mdiff = sb("mdiff", [P, 8])
        mdiff2 = sb("mdiff2", [P, 8])
        csum = sb("csum", [P, 8])
        cvar = sb("cvar", [P, 8])
        vareps = [sb(f"vareps{i}", [P, 8]) for i in range(2)]
        rstd = [sb(f"rstd{i}", [P, 8]) for i in range(2)]
        nmr = [sb(f"nmr{i}", [P, 8]) for i in range(2)]
        mx = [sb(f"mx{i}", [P, G]) for i in range(2)]
        sm = [sb(f"sm{i}", [P, G]) for i in range(2)]
        rc = [sb(f"rc{i}", [P, G]) for i in range(2)]
        v8 = sb("v8", [P, 8])
        i8 = sb("i8", [P, 8], U32)
        negm = sb("negm", [P, 1])
        kept_of_chunk = sb("kept_of_chunk", [P, NCH * KEPT])
        b1_in = sb("b1_in", [E, HID])
        b1T = sb("b1T", [P, J, E])
        b2_sb = sb("b2_sb", [P, C])
        w1r = sb("w1r", [P, RING, HID])
        w2r = sb("w2r", [P, RING, HID])

        bank = [ctx.enter_context(nc.psum_tensor(f"bank{i}", [P, 512], F32)) for i in range(8)]
        ps_x, ps_q, ps_k, ps_v, ps_s, ps_o, ps_y, ps_t = bank

        x_loaded = [sem(f"x_loaded{i}") for i in range(4)]
        stored = [sem(f"stored{i}") for i in range(8)]
        kbd_moved = [sem(f"kbd_moved{i}") for i in range(2)]
        pbd_moved = [sem(f"pbd_moved{i}") for i in range(2)]
        consts_loaded = sem("consts_loaded")
        consts_set = sem("consts_set")
        ident_zero = sem("ident_zero")
        mask_zero = sem("mask_zero")
        base_ready = sem("base_ready")
        exp_primed = sem("exp_primed")
        zeroed = sem("zeroed")
        gw_turned = sem("gw_turned")
        gwT_ready = sem("gwT_ready")
        raw_ready = sem("raw_ready")
        mdiff_ready = sem("mdiff_ready")
        mdiff2_ready = sem("mdiff2_ready")
        csum_ready = sem("csum_ready")
        cvar_ready = sem("cvar_ready")
        var_ready = sem("var_ready")
        rstd_ready = sem("rstd_ready")
        nmr_ready = sem("nmr_ready")
        xn_ready = sem("xn_ready")
        xb_ready = sem("xb_ready")
        x_turned = sem("x_turned")
        xnT_ready = sem("xnT_ready")
        k_done = sem("k_done")
        q_done = sem("q_done")
        v_done = sem("v_done")
        kT_ready = sem("kT_ready")
        qT_ready = sem("qT_ready")
        v_ready = sem("v_ready")
        scored = sem("scored")
        mx_ready = sem("mx_ready")
        shifted = sem("shifted")
        exp_done = sem("exp_done")
        sm_ready = sem("sm_ready")
        rc_ready = sem("rc_ready")
        p_normed = sem("p_normed")
        pT_ready = sem("pT_ready")
        pv_done = sem("pv_done")
        oT_ready = sem("oT_ready")
        y_done = sem("y_done")
        t_ready = sem("t_ready")
        tn_ready = sem("tn_ready")
        t_turned = sem("t_turned")
        tnT_ready = sem("tnT_ready")
        gate_done = sem("gate_done")
        l_ready = sem("l_ready")
        v8_ready = sem("v8_ready")
        i8_ready = sem("i8_ready")
        negm_ready = sem("negm_ready")
        early_copied = sem("early_copied")
        chunk_kept = sem("chunk_kept")
        chunk_summed = sem("chunk_summed")
        w1_loaded = [sem(f"w1_loaded{i}") for i in range(RING)]
        w2_loaded = [sem(f"w2_loaded{i}") for i in range(RING)]
        biases_loaded = sem("biases_loaded")

        def slots(eng, step):
            for n in range(2 * CH):
                step(n, n % CH, lambda k, n=n: 0 <= n - k < NBLK, None)
            with eng.Fori(0, NCH - 2) as c:
                for u in range(CH):
                    step(CH * c + (2 * CH + u), u, lambda k: True, c)
            for n in range(NBLK, NBLK + CH + 7):
                step(n, n % CH, lambda k, n=n: 0 <= n - k < NBLK, n // CH - 2)

        def wait_uses(eng, s, n, u, k, ring, per, more=0):
            b = n - k
            if isinstance(b, int):
                if b // ring + 1 + more > 0:
                    eng.wait_ge(s[b % ring], per * (b // ring + 1 + more))
            else:
                off = 2 * CH + u - k
                c8 = n - (2 * CH + u)
                eng.wait_ge(s[off % ring], c8 * (per // ring) + per * (off // ring + 1 + more))

        def after(eng, s, value):
            if not isinstance(value, int) or value > 0:
                eng.wait_ge(s, value)

        def grouped(ap):
            return ap.rearrange("p (a g w) -> p a g w", a=16, w=2)

        def windows(ap):
            return ap.rearrange("p (g a w) -> p a g w", a=16, w=2)

        main = nc.Block()
        with main as block:

            @block.sync
            def _(sp):
                sp.dma_start(w_sb[:, :], w_qkv).then_inc(consts_loaded, 16)
                sp.dma_start(wp_sb[:, :], w_proj).then_inc(consts_loaded, 16)
                sp.dma_start(bp_sb[:, :], b_proj.rearrange("(a c) -> a c", a=1).to_broadcast([P, C]))\
                  .then_inc(consts_loaded, 16)
                sp.dma_start(gw_in[:, :], gate_w).then_inc(consts_loaded, 16)
                for h in range(2):
                    sp.dma_start(gb2[64 * h:64 * h + 64, :], gate_b.rearrange("(e a) -> e a", a=1))\
                      .then_inc(consts_loaded, 16)
                for b in range(2):
                    sp.dma_start(xin[b], x_blk[b]).then_inc(x_loaded[b], 16)

                sp.dma_start(b1_in[:, :], weight1[:, C, :]).then_inc(biases_loaded, 16)
                for h in range(2):
                    sp.dma_start(b2_sb[64 * h:64 * h + 64, :], weight2[:, HID, :]).then_inc(biases_loaded, 16)

                sp.wait_ge(zeroed, 5)

                def step(n, u, has, chunk):
                    if has(-2):
                        if has(2):
                            sp.wait_ge(xb_ready, n - 2 + 1)
                        sp.dma_start(xin[(u + 2) % 4], x_blk[bass.ds(n + 2, 1)].rearrange("a p c -> (a p) c"))\
                          .then_inc(x_loaded[(u + 2) % 4], 16)
                    if has(LN2):
                        after(sp, t_ready, n - LN2 + 1)
                        sp.dma_start(out_blk[bass.ds(n - LN2, 1)].rearrange("a p c -> (a p) c"),
                                     xt[(u - LN2) % 8]).then_inc(stored[(u - LN2) % 8], 16)
                    if has(QKV):
                        i = (u - QKV) % 2
                        if has(QKV + 2):
                            sp.wait_ge(scored, n - QKV - 2 + 1)
                        after(sp, kT_ready, n - QKV + 1)
                        for h in range(HEADS):
                            sp.dma_start(kbd[i][32 * h:32 * h + 32, 512 * h:512 * h + 512],
                                         kT[i][32 * h:32 * h + 32, :]).then_inc(kbd_moved[i], 16)
                    if has(PT):
                        i = (u - PT) % 2
                        after(sp, pT_ready, n - PT + 1)
                        for g in range(4):
                            sp.dma_start(pbd[i][32 * g:32 * g + 32, 512 * g:512 * g + 512],
                                         pT[i][32 * g:32 * g + 32, :]).then_inc(pbd_moved[i], 16)

                for n in range(2 * CH):
                    step(n, n % CH, lambda k, n=n: 0 <= n - k < NBLK, None)
                with sp.Fori(0, NCH - 3) as c:
                    for u in range(CH):
                        step(CH * c + (2 * CH + u), u, lambda k: True, None)
                for n in range(NBLK - CH, NBLK + CH):
                    step(n, n % CH, lambda k, n=n: 0 <= n - k < NBLK, None)
                    e = n - (NBLK - CH)
                    sp.dma_start(w1r[:, e, :], weight1[e, 0:C, :]).then_inc(w1_loaded[e], 16)
                    sp.dma_start(w2r[:, e, :], weight2[e, 0:HID, :].rearrange("(p a) o -> p (a o)", a=J))\
                      .then_inc(w2_loaded[e], 16)
                for i in range(8):
                    sp.wait_ge(stored[i], 16 * (NBLK // 8))

            @block.gpsimd
            def _(pool):
                pool.memset(ident[:, :], 0.0).then_inc(ident_zero, 1)
                pool.memset(arena_a[:, 4096:8192], 0.0).then_inc(zeroed, 1)
                pool.memset(arena_b[:, 0:4096], 0.0).then_inc(zeroed, 1)
                pool.memset(eps8[:, 0:4], 1e-6).then_inc(consts_set, 1)
                pool.memset(eps8[:, 4:8], 1e-5).then_inc(consts_set, 1)
                pool.memset(minus_half[:, :], -0.5).then_inc(consts_set, 1)
                pool.wait_ge(ident_zero, 1)
                pool.affine_select(out=ident[:, :], in_=ident[:, :], compare_op=ALU.not_equal, fill=1.0,
                                   base=0, pattern=[[-1, P]], channel_multiplier=1).then_inc(consts_set, 1)
                pool.wait_ge(consts_set, 4)
                pool.wait_ge(consts_loaded, 96)

                def step(n, u, has, chunk):
                    ln1, ln2 = has(0), has(LN2)
                    lo, hi = (0 if ln1 else 4), (8 if ln2 else 4)
                    i = u % 2
                    if has(XT):
                        b = xt[(u - XT) % 8].rearrange("p (j c) -> p j c", j=J)
                        if has(XT + 8):
                            wait_uses(pool, stored, n, u, XT + 8, 8, 16)
                            pool.wait_ge(tn_ready, n - XT - 8 + 1)
                        pool.wait_ge(xn_ready, n - XT + 1)
                        pool.tensor_tensor(b, xin[(u - XT) % 4].rearrange("p (j c) -> p j c", j=J),
                                           bp_sb[:, :].unsqueeze(1).to_broadcast([P, J, C]), ALU.add)\
                            .then_inc(xb_ready, 1)
                    if ln1 or ln2:
                        pool.wait_ge(var_ready, n + 1)
                        if has(2):
                            pool.wait_ge(xn_ready, n - 2 + 1)
                        if has(LN2 + 2):
                            pool.wait_ge(tn_ready, n - LN2 - 2 + 1)
                        pool.tensor_tensor(rstd[i][:, lo:hi], vareps[i][:, lo:hi], minus_half[:, lo:hi], ALU.pow)\
                            .then_inc(rstd_ready, 1)
                    if has(SM):
                        k = (u - SM) % 2
                        b = pr[k].rearrange("p (a m) -> p a m", m=32)
                        if ln2:
                            pool.wait_ge(nmr_ready, n + 1)
                            if has(LN2 + 2):
                                pool.wait_ge(t_turned, n - LN2 - 2 + 1)
                        pool.wait_ge(rc_ready, n - SM + 1)
                        pool.tensor_tensor(b, b, rc[k][:, :].unsqueeze(2).to_broadcast([P, G, 32]), ALU.mult)\
                            .then_inc(p_normed, 1)
                    if ln2:
                        t = xt[(u - LN2) % 8]
                        k = (u - LN2) % 2
                        if not has(SM):
                            pool.wait_ge(nmr_ready, n + 1)
                            pool.wait_ge(t_turned, n - LN2 - 2 + 1)
                        for j in range(J):
                            ins = pool.tensor_scalar(tn[k][:, C * j:C * j + C], t[:, C * j:C * j + C],
                                                     rstd[i][:, 4 + j:5 + j], nmr[i][:, 4 + j:5 + j],
                                                     ALU.mult, ALU.add)
                        ins.then_inc(tn_ready, 1)
                slots(pool, step)

            @block.tensor
            def _(pe):
                pe.wait_ge(consts_set, 4)
                pe.wait_ge(consts_loaded, 96)
                pe.transpose(ps_t[:, 0:E], gw_in[:, :], ident[0:E, 0:E]).then_inc(gw_turned, 1)
                pe.wait_ge(gwT_ready, 1)
                pe.wait_ge(biases_loaded, 48)
                for a in range(J):
                    ins = pe.transpose(ps_x[:, E * a:E * a + E], b1_in[:, a::J], ident[0:E, 0:E])
                ins.then_inc(gw_turned, 1)
                pe.wait_ge(gwT_ready, 2)
                pe.wait_ge(zeroed, 5)

                def step(n, u, has, chunk):
                    if has(QKV):
                        i = (u - QKV) % 2
                        pe.wait_ge(xnT_ready, n - QKV + 1)
                        after(pe, kT_ready, n - QKV)
                        pe.matmul(ps_k[:, :], w_sb[:, C:2 * C], xnT[i][:, :], start=True, stop=True)\
                          .then_inc(k_done, 1)
                    if has(XT):
                        pe.wait_ge(xn_ready, n - XT + 1)
                        after(pe, xnT_ready, n - XT)
                        for j in range(J):
                            ins = pe.transpose(ps_x[:, P * j:P * j + P], xn[(u - XT) % 2][:, P * j:P * j + P],
                                               ident[:, :])
                        ins.then_inc(x_turned, 1)
                    if has(QKV):
                        i = (u - QKV) % 2
                        after(pe, qT_ready, n - QKV)
                        pe.matmul(ps_q[:, :], w_sb[:, 0:C], xnT[i][:, :], start=True, stop=True)\
                          .then_inc(q_done, 1)
                    if has(GATE):
                        pe.wait_ge(tn_ready, n - GATE + 1)
                        after(pe, l_ready, n - GATE)
                        for j in range(J):
                            ins = pe.transpose(ps_t[:, P * j:P * j + P], tn[(u - GATE) % 2][:, P * j:P * j + P],
                                               ident[:, :])
                        ins.then_inc(t_turned, 1)
                    if has(PV):
                        i = (u - PV) % 2
                        wait_uses(pe, pbd_moved, n, u, PV, 2, 64)
                        after(pe, oT_ready, n - PV)
                        pb = pbd[i].rearrange("p (g m) -> p g m", g=4)
                        vv = v[(u - PV) % 4]
                        for t in range(J):
                            for h in range(HEADS):
                                m = P * t + HD * h
                                ins = pe.matmul(ps_o[HD * h:HD * h + HD, P * t:P * t + P], vv[:, m:m + HD],
                                                pb[:, :, m:m + 32], start=True, stop=True)
                        ins.then_inc(pv_done, 1)
                    if has(QKV):
                        i = (u - QKV) % 2
                        after(pe, v_ready, n - QKV)
                        for t in range(J):
                            ins = pe.matmul(ps_v[:, P * t:P * t + P], xnT[i][:, P * t:P * t + P],
                                            w_sb[:, 2 * C:3 * C], start=True, stop=True)
                        ins.then_inc(v_done, 1)
                    if has(SC):
                        i = (u - SC) % 2
                        wait_uses(pe, kbd_moved, n, u, SC, 2, 64)
                        pe.wait_ge(qT_ready, n - SC + 1)
                        after(pe, shifted, n - SC)
                        pe.matmul(ps_s[:, :], mask_q[:, :], mask_k[:, :], start=True, stop=False,
                                  skip_group_check=True)
                        kk = kbd[i].rearrange("p (h m) -> p h m", h=HEADS)
                        for t in range(J):
                            for g in range(4):
                                m = 32 * (4 * t + g)
                                ins = pe.matmul(ps_s[32 * g:32 * g + 32, P * t:P * t + P], qT[i][:, m:m + 32],
                                                kk[:, :, m:m + 32], start=False, stop=(t == 3),
                                                skip_group_check=True)
                        ins.then_inc(scored, 1)
                    if has(PV):
                        pe.wait_ge(oT_ready, n - PV + 1)
                        after(pe, t_ready, n - PV)
                        for j in range(J):
                            ins = pe.matmul(ps_y[:, P * j:P * j + P], oT[(u - PV) % 2][:, P * j:P * j + P],
                                            wp_sb[:, :], start=True, stop=True)
                        ins.then_inc(y_done, 1)
                    if has(GATE):
                        pe.wait_ge(tnT_ready, n - GATE + 1)
                        for hf in range(2):
                            ins = pe.matmul(ps_t[64 * hf:64 * hf + 64, 0:256], gwT[:, :],
                                            tnT[(u - GATE) % 2][:, 256 * hf:256 * hf + 256], start=True, stop=True)
                        ins.then_inc(gate_done, 1)

                slots(pe, step)

            @block.scalar
            def _(act):
                act.wait_ge(consts_set, 4)
                nc.scalar.activation(early[:, 0:1], ident[:, 0:1], ACT.Exp).then_inc(exp_primed, 1)
                act.wait_ge(exp_primed, 1)
                act.sem_inc(chunk_summed, 1)
                act.wait_ge(gw_turned, 1)
                nc.scalar.activation(gwT[:, :], ps_t[:, 0:E], ACT.Copy).then_inc(gwT_ready, 1)
                act.wait_ge(gw_turned, 2)
                nc.scalar.activation(b1T[:, :, :], ps_x[:, 0:J * E].rearrange("p (a e) -> p a e", a=J), ACT.Copy)\
                    .then_inc(gwT_ready, 1)
                act.wait_ge(gwT_ready, 2)

                def step(n, u, has, chunk):
                    if has(GATE + 1):
                        k = (u - GATE - 1) % CH
                        if k == 0 and chunk is not None:
                            act.wait_ge(early_copied, chunk + 1)
                        if k == 4 and chunk is not None:
                            act.wait_ge(chunk_summed, 2 * chunk + 2)
                        act.wait_ge(gate_done, n - GATE - 1 + 1)
                        place = early if k < 4 else logits
                        nc.scalar.activation(place[:, 256 * k:256 * k + 256], ps_t[:, 0:256], ACT.Identity,
                                             bias=gb2[:, 0:1]).then_inc(l_ready, 1)
                    if has(QKV):
                        i = (u - QKV) % 2
                        act.wait_ge(k_done, n - QKV + 1)
                        if has(QKV + 2):
                            wait_uses(act, kbd_moved, n, u, QKV + 2, 2, 64)
                        nc.scalar.activation(kT[i], ps_k[:, :], ACT.Copy).then_inc(kT_ready, 1)
                    if has(XT):
                        act.wait_ge(x_turned, n - XT + 1)
                        if has(XT + 2):
                            act.wait_ge(v_done, n - XT - 2 + 1)
                        nc.scalar.activation(windows(xnT[(u - XT) % 2]), grouped(ps_x[:, :]), ACT.Copy)\
                            .then_inc(xnT_ready, 1)
                    if has(SM):
                        act.wait_ge(shifted, n - SM + 1)
                        b = pr[(u - SM) % 2]
                        nc.scalar.activation(b, b, ACT.Exp, scale=SCALE).then_inc(exp_done, 1)
                    if has(QKV):
                        i = (u - QKV) % 2
                        act.wait_ge(q_done, n - QKV + 1)
                        if has(QKV + 2):
                            act.wait_ge(scored, n - QKV - 2 + 1)
                        nc.scalar.activation(qT[i], ps_q[:, :], ACT.Copy).then_inc(qT_ready, 1)
                    if has(GATE):
                        act.wait_ge(t_turned, n - GATE + 1)
                        if has(GATE + 2):
                            act.wait_ge(gate_done, n - GATE - 2 + 1)
                        nc.scalar.activation(
                            tnT[(u - GATE) % 2][:, :].rearrange("c (f p a) -> c a f p", f=2, a=2),
                            ps_t[:, :].rearrange("c (a f p) -> c a f p", a=2, f=2), ACT.Copy).then_inc(tnT_ready, 1)
                    if has(PV):
                        act.wait_ge(pv_done, n - PV + 1)
                        if has(PV + 2):
                            act.wait_ge(y_done, n - PV - 2 + 1)
                        nc.scalar.activation(grouped(oT[(u - PV) % 2][:, :]), windows(ps_o[:, :]), ACT.Copy)\
                            .then_inc(oT_ready, 1)
                    if has(QKV):
                        act.wait_ge(v_done, n - QKV + 1)
                        if has(QKV + 4):
                            act.wait_ge(pv_done, n - QKV - 4 + 1)
                        nc.scalar.activation(v[(u - QKV) % 4], ps_v[:, :], ACT.Copy).then_inc(v_ready, 1)
                    if has(0):
                        i = u % 2
                        act.wait_ge(nmr_ready, n + 1)
                        if has(2):
                            act.wait_ge(x_turned, n - 2 + 1)
                        for j in range(J):
                            ins = nc.scalar.activation(xn[i][:, C * j:C * j + C], xin[u % 4][:, C * j:C * j + C],
                                                       ACT.Identity, bias=nmr[i][:, j:j + 1],
                                                       scale=rstd[i][:, j:j + 1])
                        ins.then_inc(xn_ready, 1)
                    if u == 7 and has(GATE + 6):
                        act.wait_ge(l_ready, n - GATE - 3 + 1)
                        if chunk is not None:
                            act.wait_ge(chunk_summed, 2 * chunk + 3)
                        nc.scalar.activation(logits[:, 0:1024], early[:, :], ACT.Copy).then_inc(early_copied, 1)
                    for half in range(2):
                        if u == 6 - half and chunk is not None:
                            act.wait_ge(negm_ready, chunk + 1)
                            act.wait_ge(chunk_kept, chunk + 2)
                            act.wait_ge(chunk_summed, 2 * chunk + 2 - half)
                            part = logits[:, 1024 * half:1024 * half + 1024]
                            nc.scalar.activation(part, part, ACT.Exp, bias=negm[:, 0:1],
                                                 accum_out=kept_of_chunk[:, bass.ds(KEPT * chunk + 2 * K8 + half, 1)])\
                                .then_inc(chunk_summed, 1)

                slots(act, step)

            @block.vector
            def _(dve):
                dve.memset(mask_q[:, :].bitcast(U32), 0).then_inc(mask_zero, 1)
                dve.memset(mask_k[:, :].bitcast(U32), 0).then_inc(mask_zero, 1)
                dve.wait_ge(mask_zero, 2)
                for row in range(2):
                    dve.memset(mask_q[32 * row:32 * row + 1, row::2], 1.0).then_inc(zeroed, 1)
                dve.memset(mask_k[0:1, 1::2], MASKED)
                dve.memset(mask_k[32:33, 0::2], MASKED).then_inc(zeroed, 1)
                dve.memset(base[0:64, :], 0.0)
                dve.memset(base[64:128, :], 1.0).then_inc(base_ready, 1)
                dve.wait_ge(base_ready, 1)
                dve.sem_inc(chunk_kept, 1)
                dve.wait_ge(consts_set, 4)

                def step(n, u, has, chunk):
                    i = u % 2
                    ln1, ln2 = has(0), has(LN2)
                    lo, hi = (0 if ln1 else 4), (8 if ln2 else 4)
                    if has(SM):
                        k = (u - SM) % 2
                        s16 = ps_s[:, :].rearrange("p (a m) -> p a m", m=32)
                        dve.wait_ge(scored, n - SM + 1)
                        dve.tensor_reduce(mx[k][:, :], s16, X, ALU.max).then_inc(mx_ready, 1)
                        dve.wait_ge(mx_ready, n - SM + 1)
                        if has(SM + 2):
                            dve.wait_ge(pT_ready, n - SM - 2 + 1)
                        dve.tensor_tensor(pr[k].rearrange("p (a m) -> p a m", m=32), s16,
                                          mx[k][:, :].unsqueeze(2).to_broadcast([P, G, 32]), ALU.subtract)\
                           .then_inc(shifted, 1)
                    if ln1 or ln2:
                        after(dve, cvar_ready, n)
                        if ln2:
                            dve.wait_ge(t_ready, n - LN2 + 1)
                            for j in range(J):
                                ins = dve.bn_stats(raw[i][:, 4 + j, :], xt[(u - LN2) % 8][:, C * j:C * j + C])
                        if ln1:
                            wait_uses(dve, x_loaded, n, u, 0, 4, 16)
                            for j in range(J):
                                ins = dve.bn_stats(raw[i][:, j, :], xin[u % 4][:, C * j:C * j + C])
                        ins.then_inc(raw_ready, 1)
                        dve.wait_ge(raw_ready, n + 1)
                        r = raw[i]
                        after(dve, nmr_ready, n - 1)
                        dve.tensor_tensor(mean2[i][:, lo:hi], r[:, lo:hi, 1], r[:, lo:hi, 4], ALU.add)
                        dve.tensor_tensor(mdiff[:, lo:hi], r[:, lo:hi, 1], r[:, lo:hi, 4], ALU.subtract)\
                           .then_inc(mdiff_ready, 1)
                        dve.tensor_tensor(csum[:, lo:hi], r[:, lo:hi, 2], r[:, lo:hi, 5], ALU.add)\
                           .then_inc(csum_ready, 1)
                        dve.wait_ge(mdiff_ready, n + 1)
                        dve.scalar_tensor_tensor(out=mdiff2[:, lo:hi], in0=mdiff[:, lo:hi], scalar=C / 4.0,
                                                 in1=mdiff[:, lo:hi], op0=ALU.mult, op1=ALU.mult)\
                           .then_inc(mdiff2_ready, 1)
                        dve.wait_ge(csum_ready, n + 1)
                        dve.wait_ge(mdiff2_ready, n + 1)
                        dve.tensor_tensor(cvar[:, lo:hi], mdiff2[:, lo:hi], csum[:, lo:hi], ALU.add)\
                           .then_inc(cvar_ready, 1)
                        dve.wait_ge(cvar_ready, n + 1)
                        after(dve, rstd_ready, n - 1)
                        dve.scalar_tensor_tensor(out=vareps[i][:, lo:hi], in0=cvar[:, lo:hi], scalar=1.0 / C,
                                                 in1=eps8[:, lo:hi], op0=ALU.mult, op1=ALU.add)\
                           .then_inc(var_ready, 1)
                    if has(ADD):
                        dve.wait_ge(xb_ready, n - ADD + 1)
                        dve.wait_ge(y_done, n - ADD + 1)
                        b = xt[(u - ADD) % 8]
                        dve.tensor_tensor(b, ps_y[:, :], b, ALU.add).then_inc(t_ready, 1)
                    if has(PT):
                        k = (u - PT) % 2
                        dve.wait_ge(p_normed, n - PT + 1)
                        if has(PT + 2):
                            wait_uses(dve, pbd_moved, n, u, PT + 2, 2, 64)
                            dve.wait_ge(pv_done, n - PT - 2 + 1)
                        dve.transpose(pT[k], pr[k]).then_inc(pT_ready, 1)
                    if has(SM):
                        k = (u - SM) % 2
                        dve.wait_ge(exp_done, n - SM + 1)
                        dve.tensor_reduce(sm[k][:, :], pr[k].rearrange("p (a m) -> p a m", m=32), X, ALU.add)\
                           .then_inc(sm_ready, 1)
                        dve.wait_ge(sm_ready, n - SM + 1)
                        if has(SM + 2):
                            dve.wait_ge(p_normed, n - SM - 2 + 1)
                        dve.reciprocal(rc[k][:, :], sm[k][:, :]).then_inc(rc_ready, 1)
                    if u == 1 and chunk is not None:
                        dve.wait_ge(l_ready, CH * chunk + CH)
                        dve.wait_ge(early_copied, chunk + 1)
                        dve.wait_ge(chunk_kept, chunk + 1)
                    if ln1 or ln2:
                        dve.wait_ge(rstd_ready, n + 1)
                        if has(2):
                            dve.wait_ge(xn_ready, n - 2 + 1)
                        if has(LN2 + 2):
                            dve.wait_ge(tn_ready, n - LN2 - 2 + 1)
                        dve.scalar_tensor_tensor(out=nmr[i][:, lo:hi], in0=mean2[i][:, lo:hi], scalar=-0.5,
                                                 in1=rstd[i][:, lo:hi], op0=ALU.mult, op1=ALU.mult)\
                           .then_inc(nmr_ready, 1)
                    if u == 1 and chunk is not None:
                        dve.max(v8[:, :], logits[:, :]).then_inc(v8_ready, 1)
                    if u == 4 and chunk is not None:
                        dve.wait_ge(v8_ready, chunk + 1)
                        dve.wait_ge(chunk_summed, 2 * chunk + 1)
                        dve.tensor_scalar(negm[:, :], v8[:, 0:1], -1.0, None, ALU.mult).then_inc(negm_ready, 1)
                        dve.max_index(i8[:, :], v8[:, :], logits[:, :]).then_inc(i8_ready, 1)
                        dve.tensor_copy(kept_of_chunk[:, bass.ds(KEPT * chunk, K8)], v8[:, :])
                        dve.wait_ge(i8_ready, chunk + 1)
                        dve.wait_ge(base_ready, chunk + 1)
                        dve.tensor_scalar(kept_of_chunk[:, bass.ds(KEPT * chunk + K8, K8)], i8[:, :], 2.0,
                                          base[:, 0:1], ALU.mult, ALU.add).then_inc(chunk_kept, 1)
                    if u == 5 and chunk is not None:
                        dve.wait_ge(chunk_kept, chunk + 2)
                        dve.tensor_scalar(base[:, :], base[:, :], float(CH * BT), None, ALU.add)\
                           .then_inc(base_ready, 1)

                slots(dve, step)

        cand = arena_d[:, 0:PAIRS * 2 * 4 * KEPT].rearrange("p (b f m) -> p b f m", b=PAIRS, f=2)
        iota64 = sb("iota64", [P, 64])
        earlier = arena_d[:, 1152:1152 + K8 * P]
        top_m = sb("top_m", [P, PAIRS])
        rel_m = sb("rel_m", [P, PAIRS, 8])
        chunk_sum = sb("chunk_sum", [P, PAIRS, 8])
        den = sb("den", [P, PAIRS])
        rden = sb("rden", [P, PAIRS])
        top_v = sb("top_v", [P, PAIRS, K8])
        top_i = sb("top_i", [P, PAIRS, K8], U32)
        top_f = sb("top_f", [P, 64])
        top_p = sb("top_p", [P, 64])
        tokf = sb("tokf", [P, 64])
        toku = sb("toku", [P, 64], U32)
        twice = sb("twice", [P, 64])
        put_f = sb("put_f", [P, 64])
        put_u = sb("put_u", [P, 64], U32)
        g_raw = sb("g_raw", [P, 64, 6])
        g_mv = sb("g_mv", [P, 64, 2])
        g_var = sb("g_var", [P, 64])
        g_rstd = sb("g_rstd", [P, 64])
        g_coef = sb("g_coef", [P, 64])
        g_mean = sb("g_mean", [P, 64])
        g_off = sb("g_off", [P, PAIRS])
        TOKENS_AT = {2: (3,), 4: (4,), 6: (5,), 7: (6,)}
        STATS = (0, 1, 2), (3, 4, 5), (6,), (7,)
        pooled = tn[0], tn[1]
        pooledT = arena_c[:, 1024:1040 + B * E]
        hid = oT
        h_rows = tnT
        tok_rows = logits[:, 0:1024], logits[:, 1024:2048]
        hits = early
        outs = [arena_c[:, 3072 + 512 * i:3584 + 512 * i].rearrange("p (a o) -> p a o", a=J) for i in range(2)]
        expert_out = arena_c[:, 0:1024].rearrange("p (b c) -> p b c", c=C)

        tail_consts = sem("tail_consts")
        cands_moved = sem("cands_moved")
        d_step = sem("d_step")
        m_shift = sem("m_shift")
        m_exp = sem("m_exp")
        v_shift = sem("v_shift")
        v_exp = sem("v_exp")
        toku_ready = sem("toku_ready")
        gathers_in = [sem(f"gathers_in{b}") for b in range(PAIRS)]
        h_copied = sem("h_copied")
        h_turned = sem("h_turned")
        h_placed = sem("h_placed")
        g_var_ready = sem("g_var_ready")
        g_rstd_ready = sem("g_rstd_ready")
        pooled_ready = sem("pooled_ready")
        pooled_turned = sem("pooled_turned")
        pooledT_ready = sem("pooledT_ready")
        h_done = sem("h_done")
        h_biased = sem("h_biased")
        h_ready = sem("h_ready")
        o_done = sem("o_done")
        o_copied = sem("o_copied")
        o_stored = [sem(f"o_stored{i}") for i in range(2)]
        eo_loaded = sem("eo_loaded")
        eo_ready = sem("eo_ready")
        tokr_done = sem("tokr_done")
        tokr_copied = sem("tokr_copied")
        tokr_used = sem("tokr_used")
        put_ready = sem("put_ready")
        rows_done = sem("rows_done")
        rows_added = sem("rows_added")
        rows_put = sem("rows_put")

        ps_h, ps_e, ps_r, ps_w = bank[0:2], bank[2:4], bank[4:6], bank[6:8]
        kept8 = cand.rearrange("p b f (q m) -> p b (f q) m", m=KEPT)
        cand_v, cand_t = kept8[:, :, :, 0:K8], kept8[:, :, :, K8:2 * K8]
        cand_s = [kept8[:, :, :, 2 * K8 + half] for half in range(2)]
        values = arena_b[:, 0:PAIRS * 64].rearrange("p (b m) -> p b m", b=PAIRS)
        cand_m = kept8[:, :, :, 0]

        with nc.Block() as block:

            @block.sync
            def _(sp):
                for par in range(2):
                    for hf in range(2):
                        sp.dma_start(cand[64 * par:64 * par + 64, :, hf, :],
                                     kept_of_chunk[64 * hf:64 * hf + 64, :]
                                     .rearrange("p (b r m) -> p b r m", r=2, m=4 * KEPT)[:, :, par, :])\
                          .then_inc(cands_moved, 16)
                for g in range(RING // 8, NE):
                    for e in range(8 * g, 8 * g + 8):
                        if e % 4 == 0:
                            sp.wait_ge(h_done, (e - RING) // 4 + 1)
                        sp.dma_start(w1r[:, e % RING, :], weight1[e, 0:C, :]).then_inc(w1_loaded[e % RING], 16)
                    sp.wait_ge(o_done, g - RING // 8 + 1)
                    for e in range(8 * g, 8 * g + 8):
                        sp.dma_start(w2r[:, e % RING, :], weight2[e, 0:HID, :].rearrange("(p a) o -> p (a o)", a=J))\
                          .then_inc(w2_loaded[e % RING], 16)
                for i in range(2):
                    sp.wait_ge(o_stored[i], 128)
                for par in range(2):
                    sp.dma_start(expert_out[64 * par:64 * par + 64, :, :],
                                 expert_dram.rearrange("(b r) e o -> r e b o", r=2)[par])\
                      .then_inc(eo_loaded, 16)

            @block.gpsimd
            def _(pool):
                pool.iota(iota64[:, :], pattern=[[1, 64]], base=0, channel_multiplier=0,
                          allow_small_or_imprecise_dtypes=True).then_inc(tail_consts, 1)
                pool.memset(earlier[:, :], 1.0).then_inc(tail_consts, 1)
                pool.wait_ge(tail_consts, 2)
                last = earlier[:, (K8 - 1) * P:]
                pool.affine_select(out=last, in_=last, compare_op=ALU.is_gt, fill=0.0, base=0,
                                   pattern=[[-1, P]], channel_multiplier=1).then_inc(tail_consts, 1)

                def gather(b):
                    pool.wait_ge(toku_ready, b + 1)
                    for n in range(K8 * b, K8 * b + K8):
                        pool.indirect_dma_start(gathered[:, n, :], None, out_rows,
                                                bass.IndirectOffsetOnAxis(ap=toku[:, n:n + 1], axis=0))\
                            .then_inc(gathers_in[b], 16)

                def rstd_of(i):
                    n = slice(K8 * STATS[i][0], K8 * STATS[i][-1] + K8)
                    pool.wait_ge(g_var_ready, i + 1)
                    pool.tensor_tensor(g_rstd[:, n], g_var[:, n], minus_half[:, n], ALU.pow)\
                        .then_inc(g_rstd_ready, 1)

                for b in range(PAIRS):
                    gather(b)
                    if b == 4:
                        rstd_of(0)
                    if b == 6:
                        rstd_of(1)
                rstd_of(2)
                rstd_of(3)
                for g in range(NE):
                    pool.wait_ge(h_placed, 2 * g + 2)
                    hv = hid[g % 2][:, :].rearrange("p (e a b) -> p e a b", e=8, a=J)
                    pool.tensor_tensor(hv, hv, b1T[:, :, 8 * g:8 * g + 8].rearrange("p a e -> p e a").unsqueeze(3)
                                       .to_broadcast([P, 8, J, B]), ALU.add).then_inc(h_biased, 1)
                for b in range(PAIRS):
                    for q in range(2):
                        pool.wait_ge(rows_added, 2 * b + q + 1)
                        if q == 0:
                            pool.wait_ge(put_ready, b + 1)
                        for k in range(4):
                            n = K8 * b + 4 * q + k
                            pool.indirect_dma_start(out_rows, bass.IndirectOffsetOnAxis(ap=put_u[:, n:n + 1], axis=0),
                                                    gathered[:, n, :], None, bounds_check=B * S - 1,
                                                    oob_is_err=False).then_inc(rows_put, 16)
                pool.wait_ge(rows_put, 64 * 16)

            @block.vector
            def _(dve):
                count = [0]

                def keep(ins):
                    count[0] += 1
                    ins.then_inc(d_step, 1)

                def kept():
                    dve.wait_ge(d_step, count[0])

                dve.wait_ge(tail_consts, 3)
                dve.wait_ge(cands_moved, 4 * 16)
                keep(dve.tensor_tensor(chunk_sum[:, :, :], cand_s[0], cand_s[1], ALU.add))
                keep(dve.tensor_copy(values.rearrange("p b (c k) -> p b c k", k=K8), cand_v))
                keep(dve.tensor_reduce(top_m[:, :], cand_m, X, ALU.max))
                kept()
                dve.tensor_tensor(rel_m[:, :, :], cand_m, top_m[:, :].unsqueeze(2).to_broadcast([P, PAIRS, 8]),
                                  ALU.subtract).then_inc(m_shift, 1)
                for b in range(PAIRS):
                    ins = dve.max(top_v[:, b, :], values[:, b, :])
                keep(ins)
                kept()
                for b in range(PAIRS):
                    ins = dve.max_index(top_i[:, b, :], top_v[:, b, :], values[:, b, :])
                keep(ins)
                kept()
                keep(dve.tensor_copy(top_f[:, :], top_i[:, :, :].rearrange("p b k -> p (b k)")))
                kept()
                for b in range(PAIRS):
                    o = onehot[:, K8 * b:K8 * b + K8, :]
                    n = slice(K8 * b, K8 * b + K8)
                    keep(dve.tensor_tensor(o, iota64[:, :].unsqueeze(1).to_broadcast([P, K8, 64]),
                                           top_f[:, n].unsqueeze(2).to_broadcast([P, K8, 64]), ALU.is_equal))
                    kept()
                    oc = o.rearrange("p k (c m) -> p k c m", m=K8)
                    keep(dve.tensor_tensor(oc, oc, cand_t[:, b, :, :].unsqueeze(1).to_broadcast([P, K8, 8, K8]),
                                           ALU.mult))
                    kept()
                    keep(dve.tensor_reduce(tokf[:, n], o, X, ALU.add))
                    kept()
                    dve.tensor_copy(toku[:, n], tokf[:, n]).then_inc(toku_ready, 1)
                tv = top_v[:, :, :]
                dve.tensor_tensor(top_p[:, :].rearrange("p (b k) -> p b k", k=K8), tv,
                                  top_m[:, :].unsqueeze(2).to_broadcast([P, PAIRS, K8]), ALU.subtract)\
                   .then_inc(v_shift, 1)
                dve.wait_ge(m_exp, 1)
                keep(dve.tensor_tensor(rel_m[:, :, :], rel_m[:, :, :], chunk_sum[:, :, :], ALU.mult))
                kept()
                keep(dve.tensor_reduce(den[:, :], rel_m[:, :, :], X, ALU.add))
                kept()
                keep(dve.reciprocal(rden[:, :], den[:, :]))
                kept()
                dve.wait_ge(v_exp, 1)
                tp = top_p[:, :].rearrange("p (b k) -> p b k", k=K8)
                keep(dve.tensor_tensor(tp, tp, rden[:, :].unsqueeze(2).to_broadcast([P, PAIRS, K8]), ALU.mult))
                kept()

                def stats(i):
                    n0, n1 = K8 * STATS[i][0], K8 * STATS[i][-1] + K8
                    for b in STATS[i]:
                        dve.wait_ge(gathers_in[b], K8 * 16)
                    for n in range(n0, n1):
                        ins = dve.bn_stats(g_raw[:, n, :], gathered[:, n, :])
                    keep(ins)
                    kept()
                    for n in range(n0, n1):
                        ins = dve.bn_aggr(g_mv[:, n, :], g_raw[:, n, :])
                    keep(ins)
                    kept()
                    dve.tensor_scalar(g_var[:, n0:n1], g_mv[:, n0:n1, 1], 1e-5, None, ALU.add)\
                       .then_inc(g_var_ready, 1)

                def pool_rows(i):
                    n0, n1 = K8 * STATS[i][0], K8 * STATS[i][-1] + K8
                    b0, b1 = STATS[i][0], STATS[i][-1] + 1
                    dve.wait_ge(g_rstd_ready, i + 1)
                    keep(dve.tensor_tensor(g_coef[:, n0:n1], g_rstd[:, n0:n1], top_p[:, n0:n1], ALU.mult))
                    kept()
                    keep(dve.scalar_tensor_tensor(out=g_mean[:, n0:n1], in0=g_mv[:, n0:n1, 0], scalar=-1.0,
                                                  in1=g_coef[:, n0:n1], op0=ALU.mult, op1=ALU.mult))
                    kept()
                    keep(dve.tensor_reduce(g_off[:, b0:b1], g_mean[:, n0:n1].rearrange("p (b k) -> p b k", k=K8),
                                           X, ALU.add))
                    kept()
                    for k in range(K8):
                        for b in STATS[i]:
                            n = K8 * b + k
                            dst = pooled[b // 4][:, C * (b % 4):C * (b % 4) + C]
                            if k == 0:
                                ins = dve.tensor_scalar(dst, gathered[:, n, :], g_coef[:, n:n + 1],
                                                        g_off[:, b:b + 1], ALU.mult, ALU.add)
                            else:
                                ins = dve.scalar_tensor_tensor(out=dst, in0=gathered[:, n, :],
                                                               scalar=g_coef[:, n:n + 1], in1=dst,
                                                               op0=ALU.mult, op1=ALU.add)
                        if k < K8 - 1:
                            keep(ins)
                            kept()
                    ins.then_inc(pooled_ready, 1)

                def select(b, ranks=range(K8)):
                    rows = tok_rows[b % 2]
                    dve.wait_ge(tokr_copied, b + 1)
                    for k in ranks:
                        n = K8 * b + k
                        dst = wsel[:, b, :] if k == 0 else hits[:, :]
                        keep(dve.tensor_scalar(dst, rows, tokf[:, n:n + 1], top_p[:, n:n + 1],
                                               ALU.is_equal, ALU.mult))
                        if k:
                            kept()
                            keep(dve.tensor_tensor(wsel[:, b, :], wsel[:, b, :], hits[:, :], ALU.add))
                            kept()

                def find_first(b):
                    rows = tok_rows[b % 2]
                    for k in range(K8):
                        n = K8 * b + k
                        m = P * (k + 1)
                        ins = dve.scalar_tensor_tensor(out=hits[:, 0:m], in0=rows[:, 0:m], scalar=tokf[:, n:n + 1],
                                                       in1=earlier[:, P * K8 - m:], op0=ALU.is_equal, op1=ALU.mult,
                                                       accum_out=twice[:, n:n + 1])
                        keep(ins)
                        kept()
                    n = slice(K8 * b, K8 * b + K8)
                    put = dve.scalar_tensor_tensor(out=put_f[:, n], in0=twice[:, n], scalar=float(2 * B * S),
                                                   in1=tokf[:, n], op0=ALU.mult, op1=ALU.add)
                    put.then_inc(tokr_used, 1)
                    dve.wait_ge(tokr_used, b + 1)
                    dve.tensor_copy(put_u[:, n], put_f[:, n]).then_inc(put_ready, 1)

                def add_rows(b):
                    for q in range(2):
                        n = K8 * b + 4 * q
                        dve.wait_ge(rows_done, 2 * b + q + 1)
                        rows = gathered[:, n:n + 4, :].rearrange("p n c -> p (n c)")
                        dve.tensor_tensor(rows, ps_r[q][:, :], rows, ALU.add).then_inc(rows_added, 1)

                select(0)
                stats(0)
                find_first(0)
                pool_rows(0)
                stats(1)
                select(1, range(0, 4))
                pool_rows(1)
                stats(2)
                stats(3)
                pool_rows(2)
                pool_rows(3)
                select(1, range(4, K8))
                find_first(1)
                for b in range(2, 5):
                    select(b)
                    find_first(b)
                select(5)
                dve.wait_ge(eo_loaded, 32)
                dve.tensor_tensor(expert_out[:, :, :], expert_out[:, :, :],
                                  b2_sb[:, :].unsqueeze(1).to_broadcast([P, PAIRS, C]), ALU.add)\
                   .then_inc(eo_ready, 1)
                add_rows(0)
                add_rows(1)
                find_first(5)
                add_rows(2)
                select(6, range(0, 4))
                add_rows(3)
                select(6, range(4, K8))
                add_rows(4)
                find_first(6)
                add_rows(5)
                select(7, range(0, 4))
                add_rows(6)
                select(7, range(4, K8))
                find_first(7)
                add_rows(7)

            @block.scalar
            def _(act):
                act.wait_ge(m_shift, 1)
                nc.scalar.activation(rel_m[:, :, :], rel_m[:, :, :], ACT.Exp).then_inc(m_exp, 1)
                act.wait_ge(v_shift, 1)
                nc.scalar.activation(top_p[:, :], top_p[:, :], ACT.Exp).then_inc(v_exp, 1)

                def rows_of_tokens(b):
                    if b >= 2:
                        act.wait_ge(tokr_used, b - 1)
                    for q in range(2):
                        act.wait_ge(tokr_done, 2 * b + q + 1)
                        ins = nc.scalar.activation(tok_rows[b % 2][:, 512 * q:512 * q + 512], ps_w[q][:, :], ACT.Copy)
                    ins.then_inc(tokr_copied, 1)

                for b in range(3):
                    rows_of_tokens(b)
                for q in range(2):
                    act.wait_ge(pooled_turned, q + 1)
                    nc.scalar.activation(
                        pooledT[:, 0:B * E].rearrange("p (e m) -> p e m", m=B)[:, :, 8 * q:8 * q + 8],
                        ps_e[q][:, :].rearrange("p (m e) -> p e m", e=E), ACT.Copy).then_inc(pooledT_ready, 1)
                nc.scalar.activation(pooledT[:, B * E:], ident[:, 0:B], ACT.Copy).then_inc(pooledT_ready, 1)

                for g in range(NE):
                    for h in range(2):
                        act.wait_ge(h_done, 2 * g + h + 1)
                        if g:
                            act.wait_ge(h_turned, 2 * (g - 1) + h + 1)
                        nc.scalar.activation(h_rows[h][:, :], ps_h[h][:, :], ACT.Copy).then_inc(h_copied, 1)
                    for h in range(2):
                        act.wait_ge(h_turned, 2 * g + h + 1)
                        if g >= 2:
                            act.wait_ge(o_done, g - 1)
                        nc.scalar.activation(
                            hid[g % 2][:, 256 * h:256 * h + 256].rearrange("p (q a b) -> p q a b", q=4, a=J),
                            ps_r[h][:, :].rearrange("p (a q d b) -> p q a d b", a=J, q=4, d=2)[:, :, :, 0, :],
                            ACT.Copy).then_inc(h_placed, 1)
                    for b in TOKENS_AT.get(g, ()):
                        rows_of_tokens(b)
                    act.wait_ge(h_biased, g + 1)
                    nc.scalar.activation(hid[g % 2][:, :], hid[g % 2][:, :], ACT.Gelu).then_inc(h_ready, 1)
                    if g % 2:
                        big = g // 2
                        act.wait_ge(o_done, g + 1)
                        if big >= 2:
                            act.wait_ge(o_stored[big % 2], 64)
                        for q in range(4):
                            nc.scalar.activation(outs[big % 2][32 * q:32 * q + B, :, :].rearrange("p a o -> p (a o)"),
                                                 ps_e[big % 2][32 * q:32 * q + B, :], ACT.Copy).then_inc(o_copied, 1)
                        act.wait_ge(o_copied, 4 * (big + 1))
                        for q in range(4):
                            act.dma_start(expert_dram[:, 16 * big + q:16 * big + 16:4, :],
                                          outs[big % 2][32 * q:32 * q + B, :, :]).then_inc(o_stored[big % 2], 16)
                rows_of_tokens(PAIRS - 1)

            @block.tensor
            def _(pe):
                pe.wait_ge(toku_ready, PAIRS)

                def rows_of_tokens(b):
                    for q in range(2):
                        if b:
                            pe.wait_ge(tokr_copied, b)
                        for k in range(4):
                            n = K8 * b + 4 * q + k
                            ins = pe.matmul(ps_w[q][:, P * k:P * k + P], tokf[:, n:n + 1].to_broadcast([P, P]),
                                            ident[:, :], start=True, stop=True)
                        ins.then_inc(tokr_done, 1)

                def hidden(g):
                    for h in range(2):
                        if g:
                            pe.wait_ge(h_copied, 2 * (g - 1) + h + 1)
                        for q in range(4):
                            e = 8 * g + 4 * h + q
                            pe.wait_ge(w1_loaded[e % RING], 16 * (e // RING + 1))
                            ins = pe.matmul(ps_h[h][32 * q:32 * q + 32, :],
                                            pooledT[:, B * e:B * e + 32], w1r[:, e % RING, :], start=True, stop=True)
                        ins.then_inc(h_done, 1)

                def turn_hidden(g):
                    for h in range(2):
                        pe.wait_ge(h_copied, 2 * g + h + 1)
                        if g:
                            pe.wait_ge(h_placed, 2 * (g - 1) + h + 1)
                        for a in range(J):
                            ins = pe.transpose(ps_r[h][:, P * a:P * a + P], h_rows[h][:, a::J], ident[:, :])
                        ins.then_inc(h_turned, 1)

                def expert_rows(g):
                    pe.wait_ge(h_ready, g + 1)
                    big = g // 2
                    if g % 2 == 0 and big >= 2:
                        pe.wait_ge(o_copied, 4 * (big - 1))
                    for m in range(8):
                        e = 8 * g + m
                        pe.wait_ge(w2_loaded[e % RING], 16 * (e // RING + 1))
                        q, col = e % 4, (e % 16) // 4
                        for a in range(J):
                            ins = pe.matmul(ps_e[big % 2][32 * q:32 * q + B, C * col:C * col + C],
                                            hid[g % 2][:, (J * m + a) * B:(J * m + a + 1) * B],
                                            w2r[:, e % RING, C * a:C * a + C], start=(a == 0), stop=(a == J - 1))
                    ins.then_inc(o_done, 1)

                for b in range(3):
                    rows_of_tokens(b)
                for q in range(2):
                    pe.wait_ge(pooled_ready, (2, 4)[q])
                    for b in range(4):
                        ins = pe.transpose(ps_e[q][:, P * b:P * b + P], pooled[q][:, C * b:C * b + C], ident[:, :])
                    ins.then_inc(pooled_turned, 1)
                pe.wait_ge(pooledT_ready, 3)
                hidden(0)
                turn_hidden(0)
                for g in range(NE):
                    for b in TOKENS_AT.get(g, ()):
                        rows_of_tokens(b)
                    if g + 1 < NE:
                        hidden(g + 1)
                    expert_rows(g)
                    if g + 1 < NE:
                        turn_hidden(g + 1)
                rows_of_tokens(PAIRS - 1)
                pe.wait_ge(eo_ready, 1)
                for b in range(PAIRS):
                    pe.wait_ge(put_ready, b + 1)
                    for q in range(2):
                        if b:
                            pe.wait_ge(rows_added, 2 * (b - 1) + q + 1)
                        for k in range(4):
                            ins = pe.matmul(ps_r[q][:, C * k:C * k + C],
                                            wsel[:, b, P * (4 * q + k):P * (4 * q + k) + P],
                                            expert_out[:, b, :], start=True, stop=True)
                        ins.then_inc(rows_done, 1)


_INS = ["x", "L0_conv_w_qkv", "L0_conv_w_proj", "L0_conv_b_proj", "L0_ffn_gate_w", "L0_ffn_gate_b",
        "L0_ffn_weight1", "L0_ffn_weight2"]


def kernel(**inputs):
    import numpy as _np
    import concourse.bacc as _bacc
    from concourse.bass_utils import run_bass_kernel_spmd as _run

    nc = _bacc.Bacc("TRN2", target_bir_lowering=False, num_devices=1)
    arrays, args = {}, []
    for name in _INS:
        a = _np.ascontiguousarray(inputs[name])
        arrays[f"in_{name}"] = a
        args.append(nc.dram_tensor(f"in_{name}", a.shape, mybir.dt.from_np(a.dtype), kind="ExternalInput").ap())
    args.append(nc.dram_tensor("out_0", inputs["x"].shape, F32, kind="ExternalOutput").ap())
    metaformer_layer(nc, *args)
    r = _run(nc, [arrays], core_ids=[0])
    return r.results[0]["out_0"]
```
